# Optimizing a Trainium2 kernel written in Bass

```python
import numpy as np
import jax
import jax.numpy as jnp

def _softmax(x, axis=-1):
    return jax.nn.softmax(x, axis=axis)

def _gelu(x):
    return jax.nn.gelu(x, approximate=True)

def _silu(x):
    return jax.nn.silu(x)

def _sigmoid(x):
    return jax.nn.sigmoid(x)

def _layernorm(x, axis=-1, eps=1e-05):
    m = jnp.mean(x, axis=axis, keepdims=True)
    v = jnp.var(x, axis=axis, keepdims=True)
    return (x - m) / jnp.sqrt(v + eps)

def _scatter_add(tgt, idx, src, axis=0):
    return tgt.at[idx].add(src)

def _segment_sum(src, seg, n):
    return jax.ops.segment_sum(src, seg, n)
kernel_name = 'mk_gps_d1_gnn_r8_05a2e4'

def setup_inputs(seed: int=0):
    np.random.seed(seed)
    _w = jnp.asarray

    def _rec_inputs():
        import jax
        import jax.numpy as jnp
        _gk = jax.random.key(seed)
        x = -0.0002117 + 1 * jax.random.normal(jax.random.fold_in(_gk, 1), (6250, 256), jnp.float32)
        _s = jax.random.randint(jax.random.fold_in(_gk, 2), (50000,), 0, 6250, jnp.int32)
        _d = jax.random.randint(jax.random.fold_in(_gk, 3), (50000,), 0, 6250, jnp.int32)
        _loop = jnp.arange(6250, dtype=jnp.int32)
        src = jnp.concatenate([_s, _d, _loop])
        dst = jnp.concatenate([_d, _s, _loop])
        _o = jnp.argsort(dst, stable=True)
        src = src[_o]
        dst = dst[_o]
        return (x, src, dst)
    x, src, dst = _rec_inputs()

    def _L0_gnn_setup():
        import jax, jax.numpy as jnp
        import numpy as np
        N_NODES = 12500
        F_DIM = 256
        NNZ = 200000

        def _prelu(x, a):
            return jnp.where(x >= 0, x, a * x)

        def _hconv(x, W, b, src, dst, n):
            xt = x @ W
            ones = jnp.ones(src.shape, xt.dtype)
            D = jax.ops.segment_sum(ones, src, num_segments=n)
            B = jax.ops.segment_sum(ones, dst, num_segments=n)
            Dinv = jnp.where(D > 0, 1.0 / D, 0.0)
            Binv = jnp.where(B > 0, 1.0 / B, 0.0)
            m = jax.ops.segment_sum(xt[src], dst, num_segments=n) * Binv[:, None]
            out = jax.ops.segment_sum(m[dst], src, num_segments=n) * Dinv[:, None]
            return out + b
        key = jax.random.key(seed)
        k0, k1, k2, k3 = jax.random.split(key, 4)
        x = jax.random.normal(k0, (N_NODES, F_DIM), dtype=jnp.float32)
        edge_index = jax.random.randint(k1, (2, NNZ), 0, N_NODES, dtype=jnp.int32)
        scale = (2.0 / F_DIM) ** 0.5
        W1 = jax.random.normal(k2, (F_DIM, F_DIM), dtype=jnp.float32) * scale
        W2 = jax.random.normal(k3, (F_DIM, F_DIM), dtype=jnp.float32) * scale
        b1 = jnp.zeros((F_DIM,), jnp.float32)
        b2 = jnp.zeros((F_DIM,), jnp.float32)
        a = jnp.full((1,), 0.25, jnp.float32)
        return {'x': x, 'edge_index': edge_index, 'W1': W1, 'b1': b1, 'W2': W2, 'b2': b2, 'a': a}
    _L0_gnn_all = _L0_gnn_setup()
    _L0_gnn_in = {k: v for k, v in _L0_gnn_all.items() if k in ('W1', 'b1', 'W2', 'b2', 'a')}
    del _L0_gnn_all

    def _L0_mix_setup():
        import jax, jax.numpy as jnp
        import numpy as np
        HEADS = 8
        DIM_HEAD = 64
        EPS = 1e-05

        def _inst_norm_lastdim(t):
            mu = jnp.mean(t, axis=-1, keepdims=True)
            var = jnp.mean(jnp.square(t - mu), axis=-1, keepdims=True)
            return (t - mu) * jax.lax.rsqrt(var + EPS)
        key = jax.random.key(seed)
        k1, k2, k3, k4 = jax.random.split(key, 4)
        b, n, dim = (4, 1024, 256)
        inner = HEADS * DIM_HEAD
        x = jax.random.normal(k1, (b, n, dim), dtype=jnp.float32)
        Wqkv = jax.random.normal(k2, (3 * inner, dim), dtype=jnp.float32) * (1.0 / np.sqrt(dim))
        Wout = jax.random.normal(k3, (dim, inner), dtype=jnp.float32) * (1.0 / np.sqrt(inner))
        bout = jax.random.normal(k4, (dim,), dtype=jnp.float32) * 0.01
        return {'x': x, 'Wqkv': Wqkv, 'Wout': Wout, 'bout': bout}
    _L0_mix_all = _L0_mix_setup()
    _L0_mix_in = {k: v for k, v in _L0_mix_all.items() if k in ('Wqkv', 'Wout', 'bout')}
    del _L0_mix_all

    def _L0_ffn_setup():
        import jax, jax.numpy as jnp
        import numpy as np
        E = 8
        K = 2
        D = 256
        H = 512
        DOUT = 256
        EPS = 1e-05
        key = jax.random.key(seed)
        ks = jax.random.split(key, 9)
        s = 0.02
        return {'x': jax.random.normal(ks[0], (4, 1024, D), jnp.float32), 'gamma': 1.0 + 0.05 * jax.random.normal(ks[1], (D,), jnp.float32), 'beta': 0.05 * jax.random.normal(ks[2], (D,), jnp.float32), 'Wr': 0.01 * jax.random.normal(ks[3], (D, E), jnp.float32), 'br': jnp.zeros((E,), jnp.float32), 'W1': s * jax.random.normal(ks[4], (E, D, H), jnp.float32), 'b1': s * jax.random.normal(ks[5], (E, H), jnp.float32), 'W2': s * jax.random.normal(ks[6], (E, H, DOUT), jnp.float32), 'b2': s * jax.random.normal(ks[7], (E, DOUT), jnp.float32)}
    _L0_ffn_all = _L0_ffn_setup()
    _L0_ffn_in = {k: v for k, v in _L0_ffn_all.items() if k in ('gamma', 'beta', 'Wr', 'br', 'W1', 'b1', 'W2', 'b2')}
    del _L0_ffn_all
    return {'x': x, 'src': src, 'dst': dst, 'L0_gnn_W1': _L0_gnn_in['W1'], 'L0_gnn_b1': _L0_gnn_in['b1'], 'L0_gnn_W2': _L0_gnn_in['W2'], 'L0_gnn_b2': _L0_gnn_in['b2'], 'L0_gnn_a': _L0_gnn_in['a'], 'L0_mix_Wqkv': _L0_mix_in['Wqkv'], 'L0_mix_Wout': _L0_mix_in['Wout'], 'L0_mix_bout': _L0_mix_in['bout'], 'L0_ffn_gamma': _L0_ffn_in['gamma'], 'L0_ffn_beta': _L0_ffn_in['beta'], 'L0_ffn_Wr': _L0_ffn_in['Wr'], 'L0_ffn_br': _L0_ffn_in['br'], 'L0_ffn_W1': _L0_ffn_in['W1'], 'L0_ffn_b1': _L0_ffn_in['b1'], 'L0_ffn_W2': _L0_ffn_in['W2'], 'L0_ffn_b2': _L0_ffn_in['b2']}

def reference(x, src, dst, L0_gnn_W1, L0_gnn_b1, L0_gnn_W2, L0_gnn_b2, L0_gnn_a, L0_mix_Wqkv, L0_mix_Wout, L0_mix_bout, L0_ffn_gamma, L0_ffn_beta, L0_ffn_Wr, L0_ffn_br, L0_ffn_W1, L0_ffn_b1, L0_ffn_W2, L0_ffn_b2):
    import jax
    import jax.numpy as jnp

    def _L0_gnn_ref(x, edge_index, W1, b1, W2, b2, a):
        import jax, jax.numpy as jnp
        import numpy as np
        N_NODES = 12500
        F_DIM = 256
        NNZ = 200000

        def _prelu(x, a):
            return jnp.where(x >= 0, x, a * x)

        def _hconv(x, W, b, src, dst, n):
            xt = x @ W
            ones = jnp.ones(src.shape, xt.dtype)
            D = jax.ops.segment_sum(ones, src, num_segments=n)
            B = jax.ops.segment_sum(ones, dst, num_segments=n)
            Dinv = jnp.where(D > 0, 1.0 / D, 0.0)
            Binv = jnp.where(B > 0, 1.0 / B, 0.0)
            m = jax.ops.segment_sum(xt[src], dst, num_segments=n) * Binv[:, None]
            out = jax.ops.segment_sum(m[dst], src, num_segments=n) * Dinv[:, None]
            return out + b
        src, dst = (edge_index[0], edge_index[1])
        n = x.shape[0]
        h = _prelu(_hconv(x, W1, b1, src, dst, n), a)
        h = _hconv(h, W2, b2, src, dst, n) + x
        return _prelu(h, a)

    def _L0_mix_ref(x, Wqkv, Wout, bout):
        import jax, jax.numpy as jnp
        import numpy as np
        HEADS = 8
        DIM_HEAD = 64
        EPS = 1e-05

        def _inst_norm_lastdim(t):
            mu = jnp.mean(t, axis=-1, keepdims=True)
            var = jnp.mean(jnp.square(t - mu), axis=-1, keepdims=True)
            return (t - mu) * jax.lax.rsqrt(var + EPS)
        b, n, dim = x.shape
        qkv = jnp.einsum('bnc,fc->bnf', x, Wqkv)
        q, k, v = jnp.split(qkv, 3, axis=-1)

        def to_heads(t):
            return t.reshape(b, n, HEADS, DIM_HEAD).transpose(0, 2, 1, 3)
        q, k, v = (to_heads(q), to_heads(k), to_heads(v))
        k = _inst_norm_lastdim(k)
        v = _inst_norm_lastdim(v)
        dots = jnp.einsum('bhnd,bhne->bhde', k, v)
        out = jnp.einsum('bhnd,bhde->bhne', q, dots) / n
        out = out.transpose(0, 2, 1, 3).reshape(b, n, HEADS * DIM_HEAD)
        return jnp.einsum('bnf,cf->bnc', out, Wout) + bout

    def _L0_ffn_ref(x, gamma, beta, Wr, br, W1, b1, W2, b2):
        import jax, jax.numpy as jnp
        import numpy as np
        E = 8
        K = 2
        D = 256
        H = 512
        DOUT = 256
        EPS = 1e-05
        mu = jnp.mean(x, axis=-1, keepdims=True)
        var = jnp.mean(jnp.square(x - mu), axis=-1, keepdims=True)
        xn = (x - mu) * jax.lax.rsqrt(var + EPS) * gamma + beta
        logits = jnp.einsum('bsd,de->bse', xn, Wr) + br
        top_vals, top_idx = jax.lax.top_k(logits, K)
        w = jax.nn.softmax(top_vals, axis=-1)
        w_full = jnp.einsum('bsk,bske->bse', w, jax.nn.one_hot(top_idx, E, dtype=w.dtype))
        y = jnp.zeros(x.shape[:-1] + (DOUT,), x.dtype)
        for e in range(E):
            h = jax.nn.gelu(jnp.einsum('bsd,dh->bsh', xn, W1[e]) + b1[e], approximate=False)
            y_e = jnp.einsum('bsh,hd->bsd', h, W2[e]) + b2[e]
            y = y + y_e * w_full[..., e, None]
        return y
    edge_index = jnp.stack([src, dst])
    xn = _layernorm(x, axis=-1)
    x = x + _L0_gnn_ref(xn, edge_index, L0_gnn_W1, L0_gnn_b1, L0_gnn_W2, L0_gnn_b2, L0_gnn_a) + _L0_mix_ref(xn[None], L0_mix_Wqkv, L0_mix_Wout, L0_mix_bout)[0]
    x = x + _L0_ffn_ref(_layernorm(x, axis=-1)[None], L0_ffn_gamma, L0_ffn_beta, L0_ffn_Wr, L0_ffn_br, L0_ffn_W1, L0_ffn_b1, L0_ffn_W2, L0_ffn_b2)[0]
    return x

_drawn_inputs = setup_inputs


def setup_inputs(seed=0):
    import zlib

    import numpy as np

    out = dict(_drawn_inputs(seed))
    spreads = {'L0_gnn_b1': (0.0, 0.1), 'L0_gnn_b2': (0.0, 0.1), 'L0_ffn_br': (0.0, 0.1)}
    factors = {'L0_gnn_W1': 5.358,
     'L0_mix_bout': 8.0,
     'L0_ffn_gamma': 8.0,
     'L0_ffn_beta': 8.0,
     'L0_ffn_b1': 8.0,
     'L0_ffn_b2': 7.431}
    for name, (base, spread) in spreads.items():
        noise = np.random.default_rng([zlib.crc32(name.encode()), seed]).standard_normal(out[name].shape)
        drawn = base * np.exp(spread * noise) if base else spread * noise
        out[name] = jnp.asarray(drawn.astype(out[name].dtype))
    for name, factor in factors.items():
        out[name] = (out[name] * factor).astype(out[name].dtype)
    return out
```

```python
import concourse.bass as bass
from concourse import mybir
from contextlib import ExitStack

P = 128


class Chain:

    def __init__(self, engine, semaphore):
        self.engine, self.semaphore, self.count, self.step = engine, semaphore, 0, None

    def __call__(self, instruction):
        instruction.then_inc(self.semaphore, 1)
        self.count += 1
        self.engine.wait_ge(self.semaphore, self.count if self.step is None else self.step + self.count)

    def enter(self, i, per_turn):
        self.step, self.per_turn, self.at_entry = i * per_turn, per_turn, self.count

    def leave(self, turns):
        assert self.count - self.at_entry == self.per_turn, (self.count - self.at_entry, self.per_turn)
        self.count, self.step = self.at_entry + self.per_turn * turns, None


def gps_layer(nc, x, src, dst, gnn_w1, gnn_b1, gnn_w2, gnn_b2, gnn_a, wqkv, wout, bout,
              gamma, beta, wr, br, ffn_w1, ffn_b1, ffn_w2, ffn_b2, out):
    f32, i32, f16 = mybir.dt.float32, mybir.dt.int32, mybir.dt.float16
    u16, u32 = mybir.dt.uint16, mybir.dt.uint32
    ALU, ACT, AX = mybir.AluOpType, mybir.ActivationFunctionType, mybir.AxisListType
    DVE = mybir.EngineType.DVE
    ds = bass.ds
    N, F = x.shape
    E = src.shape[0]
    KT = F // P
    NB = -(-N // P)
    LAST = N - (NB - 1) * P
    COLS, REST = E // P, E % P
    U = 16
    EC = -(-(COLS + 1) // U) * U
    NC = -(-((E + NB * (P - 1)) // P) // U) * U
    HC = NC // 2
    NW = -(-NC // P)
    TURNS, SORT_TURNS = NC // U, EC // U
    FC = F + 1
    AB = 4
    LEAD = 3
    NO_CHUNK = 2048
    R7 = 7
    NR7 = NB // R7
    HEADS, DH = 8, 64
    INNER = HEADS * DH
    PAIRS = INNER // P
    EPS = 1e-5
    NE, D, H = ffn_w1.shape
    HT = H // P
    G = 4
    LINKS = 66
    NG = NB // G
    assert NB % R7 == 0 and NB == NG * G + 1 and NG % 2 == 0 and SORT_TURNS % 2 == 0 and HC <= 512
    assert NB < SORT_TURNS and NB < TURNS

    ctx = ExitStack()
    with ctx:
        def sb(name, shape, dt):
            return ctx.enter_context(nc.sbuf_tensor(name, shape, dt))

        def sem(name):
            return ctx.enter_context(nc.semaphore(name))

        def dram(name, shape, dt=f32):
            return nc.dram_tensor(name, shape, dt).ap()

        ctx.enter_context(nc.allow_non_contiguous_dma("the last column of edges"))
        PS = ctx.enter_context(nc.psum_tensor("PS", [P, 8, 512], f32))

        tables = [dram(f"table{p}", (NB * P, F)) for p in range(4)]
        blk_dram = [dram(f"blk_dram{o}", (P, NW), i32) for o in range(2)]
        xpad_d = dram("xpad_d", (NB * P, F))
        xn_d = dram("xn_d", (NB * P, F))
        xt_d = dram("xt_d", (NB * P, F))
        wkv_d = dram("wkv_d", (P, KT * 2 * INNER))
        wout_d = dram("wout_d", (P, PAIRS * F))
        resid_d = dram("resid_d", (NB * P, F))
        skip_d = dram("skip_d", (NB * P, F))

        accs = [sb(f"acc{n}", [P, NB, FC], f32) for n in range(2)]
        REGION = 13000
        region = sb("region", [P, REGION], f32)
        gbuf = sb("gbuf", [P, U, FC], f32)
        ohg = sb("ohg", [P, U, P], f32)
        idx = [sb(f"idx{o}", [P, NC + U], i32) for o in range(2)]
        dl = [sb(f"dl{o}", [P, NC + U], f16) for o in range(2)]
        blk_row = [sb(f"blk_row{o}", [1, P * NW], i32) for o in range(2)]
        idxb = sb("idxb", [P, U], i32)
        iota_c = sb("iota_c", [P, NC], f16)
        iota_f = sb("iota_f", [P, P], f32)
        iota_h = sb("iota_h", [P, P], f16)
        iota_1 = sb("iota_1", [P, P], f16)
        iota_w = sb("iota_w", [P, NW], f32)
        lower = sb("lower", [P, P], f32)
        ones = sb("ones", [P, P], f32)
        ident = sb("ident", [P, P], f32)
        cen = sb("cen", [P, P], f32)
        z16 = sb("z16", [P, P], f16)
        inv = sb("inv", [P, NB], f32)
        vecs = sb("vecs", [P, 3, F], f32)
        a_col = sb("a_col", [P, 1], f32)
        gmat = sb("gmat", [P, KT, F], f32)

        def carve(base, sizes):
            views, at = {}, 0
            for name, (shape, dt) in sizes.items():
                n = 1
                for s in shape:
                    n *= s
                words = -(-n * (2 if dt in (f16, u16) else 4) // 4)
                v = base[:, at:at + words]
                if dt is not f32:
                    v = v.bitcast(dt)
                if len(shape) == 2:
                    v = v.rearrange("p (a b) -> p a b", b=shape[1])
                if len(shape) == 3:
                    v = v.rearrange("p (a b c) -> p a b c", b=shape[1], c=shape[2])
                views[name] = v
                at += words
            assert at <= base.shape[1], (at, base.shape)
            return views

        acc_flat = [a[:, :, :].rearrange("p b f -> p (b f)") for a in accs]
        gbuf_flat = gbuf[:, :, :].rearrange("p b f -> p (b f)")
        ohg_flat = ohg[:, :, :].rearrange("p b f -> p (b f)")

        r = carve(region, {
            "edges": ((2, EC), i32), "key16": ((EC,), f16), "oh16": ((2, EC), f16), "run": ((EC,), f32),
            "pos": ((EC,), f32), "ti": ((2, EC), i32), "chunk0": ((EC,), f32), "slot0": ((EC,), f32),
            "fa0": ((EC,), f32), "fb0": ((EC,), f32), "ohc": ((4, NC), f16), "ohs": ((4, P), f16),
            "ohv": ((8, P), f16), "unp": ((NC,), i32)})
        EL = EC + LEAD
        r1 = carve(acc_flat[1], {"chunk1": ((EL,), f32), "slot1": ((EL,), f32), "fa1": ((EL,), f32),
                                 "fb1": ((EL,), f32)})
        r.update(r1)
        edges, key16, oh16, run, pos, ti = (r[k] for k in ("edges", "key16", "oh16", "run", "pos", "ti"))
        chunk_of = [r["chunk0"], r["chunk1"]]
        slot_of = [r["slot0"], r["slot1"]]
        field_a = [r["fa0"], r["fa1"]]
        field_b = [r["fb0"], r["fb1"]]
        ohc, ohs, ohv = r["ohc"], r["ohs"], r["ohv"].rearrange("p (k f) n -> p k f n", f=2)
        small = sb("small", [P, 8, SORT_TURNS], f32)
        rowtot, nch, endc, base, mean_c, rstd_c, var_c, tmp_c = (small[:, k, :] for k in range(8))
        stats7, mv7 = sb("stats7", [P, R7, 6], f32), sb("mv7", [P, R7, 2], f32)
        nch_i = sb("nch_i", [P, 2, NB], i32)
        ge = sb("ge", [P, NW, NB], f32)
        bw = sb("bw", [P, NW], f32)
        bw_i = sb("bw_i", [P, NW], i32)

        x_sb = acc_flat[1][:, 0:NB * F].rearrange("p (b f) -> p b f", f=F)
        ln = carve(acc_flat[0], {
            "xn": ((R7, F), f32), "xt": ((R7, F), f32), "t1": ((R7, F), f32),             "mv": ((NB, 2), f32), "w1": ((KT, F), f32), "wkv": ((KT * 2 * INNER,), f32), "woutT": ((PAIRS * F,), f32)})
        mx = carve(region, {
            "wkv": ((KT, 2 * INNER), f32), "wq": ((PAIRS, F), f32), "woutT": ((PAIRS, F), f32),
            "sq": ((2 * HEADS, DH), f32), "kv": ((2 * HEADS, DH), f32), "xt": ((KT, P), f32),
            "dots": ((PAIRS, P), f32), "pp": ((PAIRS, F), f32), "ss": ((4, 2 * HEADS), f32),
            "xb": ((F,), f32), "xnb": ((F,), f32), "rs": ((F,), f32), "sk": ((F,), f32)})
        positive = [region[:, at:at + R7 * F].rearrange("p (b f) -> p b f", f=F)
                    for at in (0, KT * 2 * INNER + 2 * PAIRS * F)]
        raw = carve(gbuf_flat, {"wkv": ((2 * PAIRS, F), f32), "wout": ((KT, INNER), f32)})

        fr = carve(region, {"w1": ((NE, KT, H), f32), "gr": ((G, F), f32), "gT": ((KT, G * P), f32),
                            "w2g": ((KT, F), f32), "b2e": ((G, F), f32), "wr": ((KT, NE), f32),
                            "b1T": ((NE * HT,), f32), "gb": ((2, F), f32), "b1raw": ((P,), f32),
                            "br": ((NE,), f32)})
        fa_ = carve(acc_flat[0], {"w2": ((NE, HT, F), f32), "x2": ((2, G * F), f32), "ht": ((HT, G * P), f32)})
        fg = carve(gbuf_flat, {"xft": ((2, KT * G * P), f32), "y": ((2, G * F), f32)})
        fo = carve(ohg_flat, {"skip": ((G, F), f32), "resid": ((G, F), f32)})
        fs = sb("fs", [P, 440], f32)
        sm = carve(fs, {"inv": ((G,), f32), "stats": ((G, 6), f32), "mv": ((2, G, 2), f32), "rstd": ((4, G), f32),
                        "lg": ((G, NE), f32), "top": ((G, 8), f32), "topi": ((G, 8), u32), "topf": ((G, 8), f32),
                        "wts": ((6, G), f32), "oh": ((G, NE), f32), "wf": ((2, G, NE), f32), "wT": ((P,), f32)})
        xft = [fg["xft"][:, n, :].rearrange("p (k n) -> p k n", k=KT) for n in range(2)]

        s_pad, s_const, s_raw = sem("s_pad"), sem("s_const"), sem("s_raw")
        s_edges, s_x, s_w, s_vec = sem("s_edges"), sem("s_x"), sem("s_w"), sem("s_vec")
        s_dve, s_pool = sem("s_dve"), sem("s_pool")
        s_rowtot, s_cnt, s_bw = [[sem(f"{n}{o}") for o in range(2)] for n in ("s_rowtot", "s_cnt", "s_bw")]
        s_bwd, s_bwr = [[sem(f"{n}{o}") for o in range(2)] for n in ("s_bwd", "s_bwr")]
        s_ranked = [sem(f"s_ranked{o}") for o in range(2)]
        s_oh, s_ohs, s_used, s_sorted, s_idx = [[sem(f"{n}{o}") for o in range(2)]
                                                for n in ("s_oh", "s_ohs", "s_used", "s_sorted", "s_idx")]
        s_stat, s_sd, s_ln, s_xn, s_xt, s_xtc, s_t1, s_t1c, s_lnd, s_lnfree, s_xpad = [
            sem(n) for n in ("s_stat", "s_sd", "s_ln", "s_xn", "s_xt", "s_xtc", "s_t1", "s_t1c", "s_lnd", "s_lnfree", "s_xpad")]
        s_g = [sem(f"s_g{k}") for k in range(U)]
        s_idxb, s_ohg, s_mm, s_acc, s_zero, s_fin, s_tab = [
            [sem(f"{n}_{p}") for p in range(4)] for n in ("s_idxb", "s_ohg", "s_mm", "s_acc", "s_zero", "s_fin", "s_tab")]
        s_hz, s_hr = sem("s_hz"), sem("s_hr")
        s_wkv, s_wkvc, s_xtl, s_kv, s_sq, s_var, s_sdv, s_kn, s_dots = [
            sem(n) for n in ("s_wkv", "s_wkvc", "s_xtl", "s_kv", "s_sq", "s_var", "s_sdv", "s_kn", "s_dots")]
        s_dz, s_dcp, s_pp, s_ppc, s_gm, s_gmc = [sem(n) for n in ("s_dz", "s_dcp", "s_pp", "s_ppc", "s_gm", "s_gmc")]
        s_sl, s_mix, s_res, s_st = [sem(n) for n in ("s_sl", "s_mix", "s_res", "s_st")]
        s_wd, s_wl, s_b2z, s_yfree, s_settled = [sem(n) for n in ("s_wd", "s_wl", "s_b2z", "s_yfree", "s_settled")]
        s_fw, s_b1t, s_b1c = [sem(n) for n in ("s_fw", "s_b1t", "s_b1c")]
        (s_fl, s_gr, s_gt, s_gtc, s_u, s_h, s_rl, s_v1, s_d1, s_v2, s_d2, s_xf, s_xft, s_xftc, s_lg, s_lgc,
         s_e1, s_ex, s_wf, s_wt, s_wtc, s_y0, s_y0c, s_ph, s_ht, s_py, s_pyc, s_o, s_od) = [sem(n) for n in (
             "s_fl s_gr s_gt s_gtc s_u s_h s_rl s_v1 s_d1 s_v2 s_d2 s_xf s_xft s_xftc s_lg s_lgc "
             "s_e1 s_ex s_wf s_wt s_wtc s_y0 s_y0c s_ph s_ht s_py s_pyc s_o s_od").split()]
        N_CONST = 9
        N_VEC = 4 * 16
        N_FW = (8 + G) * 16

        def rows(d, b, n=1):
            return d[ds(b * P, n * P), :].rearrange("(b p) f -> p b f", p=P)

        def last_stage(engine, ahead, expert, link=None, links=0):
            def group(q, par, n, n_next):
                for e in range(NE):
                    if n_next:
                        ahead(q + 1, e, 1 - par, n_next)
                    expert(q, e, par, n)

            for step in range(NE):
                ahead(0, step, 0, G)
            with engine.Fori(0, NG // 2 - 1) as i:
                if link is not None:
                    link.enter(i, links)
                for par in range(2):
                    group(i * 2 + par, par, G, G)
            if link is not None:
                link.leave(NG // 2 - 1)
            group(NG - 2, 0, G, G)
            group(NG - 1, 1, G, 1)
            group(NG, 0, 1, 0)

        def settle(engine):
            engine.sem_inc(s_settled, 1)

        block = ctx.enter_context(nc.Block())

        @block.sync
        def _(sp):
            sp.wait_ge(s_pad, 2)
            for n, e in enumerate((dst, src)):
                sp.dma_start(edges[:, n, 0:COLS], e[0:COLS * P].rearrange("(p c) -> p c", p=P)).then_inc(s_edges, 16)
                sp.dma_start(edges[0:REST, n, COLS:COLS + 1],
                             e[COLS * P:E].rearrange("(p c) -> p c", c=1)).then_inc(s_edges, 16)
            sp.dma_start(x_sb[:, 0:NB - 1, :], rows(x, 0, NB - 1)).then_inc(s_x, 16)
            sp.dma_start(x_sb[0:LAST, NB - 1, :], x[(NB - 1) * P:N, :]).then_inc(s_x, 16)
            sp.dma_start(ln["w1"], gnn_w1.rearrange("(k p) f -> p k f", p=P)).then_inc(s_w, 16)
            for n, v in enumerate((gnn_b1, bout, gnn_b2)):
                sp.dma_start(vecs[:, n, :], v.unsqueeze(0).broadcast_to([P, F])).then_inc(s_vec, 16)
            sp.dma_start(a_col[:, :], gnn_a.unsqueeze(0).broadcast_to([P, 1])).then_inc(s_vec, 16)
            sp.wait_ge(s_x, 32)
            sp.dma_start(rows(xpad_d, 0, NB), x_sb).then_inc(s_xpad, 16)
            def chunk_blocks(o):
                sp.wait_ge(s_bw[o], 1)
                sp.dma_start(blk_dram[o], bw_i[:, :]).then_inc(s_bwd[o], 16)
                sp.wait_ge(s_bwd[o], 16)
                sp.dma_start(blk_row[o][:, :], blk_dram[o].rearrange("(a p) w -> a (p w)", a=1)).then_inc(s_bwr[o], 16)
            sp.sem_inc(s_lnfree, 1)
            sp.wait_ge(s_wkvc, 2)
            sp.dma_start(wkv_d, ln["wkv"]).then_inc(s_wd, 16)
            sp.dma_start(wout_d, ln["woutT"]).then_inc(s_wd, 16)
            with sp.Fori(0, NR7) as i:
                for k in range(R7):
                    b = i * R7 + k
                    sp.wait_ge(s_xn, i * R7 + (k + 1))
                    settle(sp)
                    sp.dma_start(xn_d[ds(b * P, P), :], ln["xn"][:, k, :]).then_inc(s_lnd, 16)
                    sp.wait_ge(s_xtc, i * R7 + (k + 1))
                    settle(sp)
                    sp.dma_start(xt_d[ds(b * P, P), :], ln["xt"][:, k, :]).then_inc(s_lnd, 16)
                    sp.wait_ge(s_t1c, i * R7 + (k + 1))
                    settle(sp)
                    sp.dma_start(tables[0][ds(b * P, P), :], ln["t1"][:, k, :]).then_inc(s_lnd, 16)
                sp.wait_ge(s_lnd, (i + 1) * (48 * R7))
                sp.sem_inc(s_lnfree, 1)
            chunk_blocks(0)
            chunk_blocks(1)

            def store_table(p):
                for n in range(NR7):
                    sp.wait_ge(s_fin[p], n + 1)
                    sp.dma_start(rows(tables[p + 1], n * R7, R7), accs[p % 2][:, n * R7:(n + 1) * R7, 0:F]).then_inc(s_tab[p], 16)

            sp.wait_ge(s_idx[1], 1)
            sp.wait_ge(s_ohs[1], EC + LEAD)
            sp.wait_ge(s_wd, 32)
            sp.dma_start(mx["wkv"].rearrange("p a b -> p (a b)"), wkv_d).then_inc(s_wl, 16)
            sp.dma_start(mx["woutT"].rearrange("p a b -> p (a b)"), wout_d).then_inc(s_wl, 16)
            sp.dma_start(mx["wq"], wqkv[0:INNER, :].rearrange("(q p) c -> p q c", p=P)).then_inc(s_wl, 16)
            store_table(0)
            with sp.Fori(0, NB) as i:
                sp.wait_ge(s_kv, i + 1)
                settle(sp)
                sp.dma_start(mx["xt"], xt_d[ds(i * P, P), :].rearrange("p (k n) -> p k n", k=KT)).then_inc(s_xtl, 16)
            store_table(1)
            sp.wait_ge(s_gm, 1)
            with sp.Fori(0, NB) as i:
                sp.dma_start(mx["xt"], xt_d[ds(i * P, P), :].rearrange("p (k n) -> p k n", k=KT)).then_inc(s_sl, 16)
                sp.dma_start(mx["xb"], xpad_d[ds(i * P, P), :]).then_inc(s_sl, 16)
                sp.dma_start(mx["xnb"], xn_d[ds(i * P, P), :]).then_inc(s_sl, 16)
                sp.wait_ge(s_res, i + 2)
                settle(sp)
                sp.dma_start(resid_d[ds(i * P, P), :], mx["rs"]).then_inc(s_st, 16)
                sp.dma_start(skip_d[ds(i * P, P), :], mx["sk"]).then_inc(s_st, 16)
                sp.wait_ge(s_st, (i + 1) * 32)
                settle(sp)
            store_table(2)
            sp.dma_start(fr["w1"], ffn_w1.rearrange("e (k p) h -> p e k h", p=P)).then_inc(s_fw, 16)
            sp.dma_start(fr["w2g"], gnn_w2.rearrange("(k p) f -> p k f", p=P)).then_inc(s_fw, 16)
            sp.wait_ge(s_b2z, 1)
            for j in range(G):
                sp.dma_start(fr["b2e"][j * NE:(j + 1) * NE, j, :], ffn_b2).then_inc(s_fw, 16)
            sp.dma_start(fr["wr"], wr.rearrange("(k p) e -> p k e", p=P)).then_inc(s_fw, 16)
            sp.dma_start(fr["b1raw"][0:NE * HT, :], ffn_b1.rearrange("e (t p) -> (e t) p", p=P)).then_inc(s_fw, 16)
            for n, v in enumerate((gamma, beta)):
                sp.dma_start(fr["gb"][:, n, :], v.unsqueeze(0).broadcast_to([P, F])).then_inc(s_fw, 16)
            sp.dma_start(fr["br"], br.unsqueeze(0).broadcast_to([P, NE])).then_inc(s_fw, 16)
            sp.wait_ge(s_tab[2], 16 * NR7)
            sp.dma_start(fa_["w2"], ffn_w2.rearrange("e (t p) f -> p e t f", p=P)).then_inc(s_fw, 16)

            def load(q, n):
                sp.dma_start(fo["skip"][:, 0:n, :], rows(skip_d, q * G, n)).then_inc(s_fl, 16)
                sp.dma_start(fo["resid"][:, 0:n, :], rows(resid_d, q * G, n)).then_inc(s_fl, 16)

            def store(q, par):
                sp.wait_ge(s_pyc, (q + 1) * NE + 1)
                settle(sp)
                sp.dma_start(rows(out, q * G, G), fg["y"][:, par, :].rearrange("p (b f) -> p b f", f=F)).then_inc(s_od, 16)
                sp.wait_ge(s_od, (q + 1) * 16)
                sp.sem_inc(s_yfree, 1)

            def turn(q, par, n_next):
                sp.wait_ge(s_v1, q + 1)
                load(q + 1, n_next)
                store(q, par)

            sp.sem_inc(s_yfree, 2)
            sp.wait_ge(s_fin[3], 1)
            load(0, G)
            with sp.Fori(0, NG // 2 - 1) as i:
                for par in range(2):
                    turn(i * 2 + par, par, G)
            turn(NG - 2, 0, G)
            turn(NG - 1, 1, 1)
            sp.wait_ge(s_pyc, (NG + 1) * NE + 1)
            sp.dma_start(out[NG * G * P:N, :], fg["y"][0:LAST, 0, 0:F]).then_inc(s_od, 16)
            sp.wait_ge(s_od, 16 * (NG + 1))
            sp.wait_ge(s_xpad, 16)

        @block.gpsimd
        def _(pool):
            link = Chain(pool, s_pool)
            gp = nc.gpsimd
            gp.memset(edges, NB * P).then_inc(s_pad, 1)
            gp.memset(x_sb[:, NB - 1, :], 0.0).then_inc(s_pad, 1)

            def iota(t, n, base, mult):
                return gp.iota(t, pattern=[[1, n]], base=base, channel_multiplier=mult, allow_small_or_imprecise_dtypes=True)

            iota(iota_f[:, :], P, 0, 0).then_inc(s_const, 1)
            iota(iota_h[:, :], P, 0, 0).then_inc(s_const, 1)
            iota(iota_1[:, :], P, 1, 0).then_inc(s_const, 1)
            iota(iota_c[:, :], NC, 0, 0).then_inc(s_const, 1)
            iota(iota_w[:, :], NW, 0, NW).then_inc(s_const, 1)
            gp.memset(ones[:, :], 1.0).then_inc(s_const, 1)
            gp.memset(z16[:, :], 0.0).then_inc(s_const, 1)
            link(gp.memset(lower[:, :], 1.0))
            link(gp.affine_select(out=lower[:, :], in_=lower[:, :], compare_op=ALU.is_gt, fill=0.0, base=0,
                                  pattern=[[1, P]], channel_multiplier=-1))
            link(gp.memset(ident[:, :], 0.0))
            gp.affine_select(out=ident[:, :], in_=ident[:, :], compare_op=ALU.not_equal, fill=1.0, base=0,
                             pattern=[[-1, P]], channel_multiplier=1).then_inc(s_const, 1)
            pool.wait_ge(s_const, 8)
            link(gp.tensor_copy(cen[:, :], ident[:, :]))
            for h in range(P // DH):
                q = cen[h * DH:(h + 1) * DH, h * DH:(h + 1) * DH]
                link(gp.tensor_scalar(q, q, -1.0 / DH, None, ALU.add))
            iota(small[:, 0, 0:1], 1, 0, 0).then_inc(s_const, 1)

            def memset_acc(p):
                gp.memset(accs[p % 2][:, :, :], 0.0).then_inc(s_zero[p], 1)

            def gather_pass(p):
                with pool.Fori(0, TURNS) as i:
                    for k in range(U):
                        if k % 8 == 0:
                            pool.wait_ge(s_idxb[p], i * 2 + (k // 8 + 1))
                        pool.wait_ge(s_mm[p], i * U + (k + 1))
                        settle(pool)
                        gp.indirect_dma_start(gbuf[:, k, 0:F], None, tables[p],
                                              bass.IndirectOffsetOnAxis(idxb[:, k:k + 1], 0)).then_inc(s_g[k], 16)

            pool.wait_ge(s_lnfree, NR7 + 1)
            pool.wait_ge(s_wd, 32)
            memset_acc(0)
            pool.wait_ge(s_wkv, 1)
            gp.memset(gbuf[:, :, F:FC], 1.0).then_inc(s_zero[0], 1)
            gather_pass(0)
            pool.wait_ge(s_idx[1], 1)
            memset_acc(1)
            pool.wait_ge(s_tab[0], 16 * NR7)
            gather_pass(1)
            memset_acc(2)
            pool.wait_ge(s_tab[1], 16 * NR7)
            gather_pass(2)
            pool.wait_ge(s_st, 32 * NB)
            gp.memset(fr["b2e"], 0.0).then_inc(s_b2z, 1)
            memset_acc(3)
            pool.wait_ge(s_tab[2], 16 * NR7)
            gather_pass(3)

        @block.scalar
        def _(act):
            A = nc.scalar.activation
            act.dma_start(raw["wkv"], wqkv[INNER:3 * INNER, :].rearrange("(q p) c -> p q c", p=P)).then_inc(s_raw, 16)
            act.dma_start(raw["wout"], wout.rearrange("(k p) h -> p k h", p=P)).then_inc(s_raw, 16)
            act.wait_ge(s_wkv, 1)
            A(ln["wkv"], PS[:, 0:4, :].rearrange("p a b -> p (a b)"), ACT.Copy).then_inc(s_wkvc, 1)
            A(ln["woutT"], PS[:, 4:6, :].rearrange("p a b -> p (a b)"), ACT.Copy).then_inc(s_wkvc, 1)
            act.wait_ge(s_stat, 1)
            act.activation(tmp_c[:, 0:NB], var_c[:, 0:NB], ACT.Sqrt).then_inc(s_sd, 1)
            act.wait_ge(s_ln, 1)
            with act.Fori(0, NR7) as i:
                act.wait_ge(s_lnfree, i + 1)
                for k in range(R7 + 2):
                    if k < R7:
                        b = i * R7 + k
                        A(ln["xn"][:, k, :], x_sb[:, ds(b, 1), :].rearrange("p a f -> p (a f)"), ACT.Identity,
                          bias=mean_c[:, ds(b, 1)], scale=rstd_c[:, ds(b, 1)]).then_inc(s_xn, 1)
                    if 1 <= k <= R7:
                        act.wait_ge(s_xt, i * R7 + k)
                        A(ln["xt"][:, k - 1, :], PS[:, 4 + (k - 1) % 2, 0:F], ACT.Copy).then_inc(s_xtc, 1)
                    if k >= 2:
                        act.wait_ge(s_t1, i * R7 + (k - 1))
                        A(ln["t1"][:, k - 2, :], PS[:, 6 + (k - 2) % 2, 0:F], ACT.Copy).then_inc(s_t1c, 1)

            def sort_column(o, i, k):
                c = i * U + k
                act.wait_ge(s_oh[o], i * U + (k + 1))
                A(ohv[:, k % 4, 0, :], ohs[:, k % 4, :], ACT.Copy, scale=field_a[o][:, ds(c, 1)])
                A(ohv[:, k % 4, 1, :], ohs[:, k % 4, :], ACT.Copy, scale=field_b[o][:, ds(c, 1)]).then_inc(s_ohs[o], 1)

            with act.Fori(0, SORT_TURNS) as i:
                for k in range(U):
                    sort_column(0, i, k)

            def row_numbers(p, i, h):
                act.wait_ge(s_mm[p], i * U + (8 * h + 8))
                nc.scalar.copy(idxb[:, 8 * h:8 * h + 8], idx[p % 2][:, ds(i * U + 8 * h, 8)]).then_inc(s_idxb[p], 1)

            def idx_pass(p, start, end, body=None):
                if start == 0:
                    if p:
                        act.wait_ge(s_idxb[p - 1], 2 * TURNS + 1)
                    row_numbers(p, 0, 0)
                with act.Fori(start, end) as i:
                    for k in range(U):
                        if k == 4:
                            row_numbers(p, i, 1)
                        if k == 12:
                            row_numbers(p, i + 1, 0)
                        if body is not None:
                            body(i, k)

            act.wait_ge(s_idx[0], 1)
            for c in range(LEAD):
                sort_column(1, 0, c)
            idx_pass(0, 0, SORT_TURNS, lambda i, k: sort_column(1, i, k + LEAD))
            idx_pass(0, SORT_TURNS, TURNS)

            act.wait_ge(s_fin[0], NR7)

            def with_kv(i, k):
                if k == 3:
                    act.wait_ge(s_kv, i + 2)
                    A(mx["sq"].rearrange("p h d -> p (h d)"), PS[:, 0:2, :].rearrange("p a b -> p (a b)"), ACT.Square).then_inc(s_sq, 1)
                if k == 9:
                    act.wait_ge(s_var, i + 1)
                    A(mx["ss"][:, 1, :], mx["ss"][:, 0, :], ACT.Sqrt).then_inc(s_sdv, 1)
            idx_pass(1, 0, NB, with_kv)
            idx_pass(1, NB, TURNS)
            for n in range(NR7):
                act.wait_ge(s_hz, n + 1)
                A(positive[n % 2], accs[1][:, n * R7:(n + 1) * R7, 0:F], ACT.Relu).then_inc(s_hr, 1)
            act.wait_ge(s_dz, 1)
            act.wait_ge(s_dots, 1)
            for q in range(PAIRS):
                for h in range(P // DH):
                    s = slice(h * DH, (h + 1) * DH)
                    m = A(mx["dots"][s, q, s], PS[s, 2, q * P + h * DH:q * P + (h + 1) * DH], ACT.Copy)
            m.then_inc(s_dcp, 1)
            act.wait_ge(s_pp, 1)
            A(mx["pp"].rearrange("p a b -> p (a b)"), PS[:, 0:2, :].rearrange("p a b -> p (a b)"), ACT.Copy).then_inc(s_ppc, 1)
            act.wait_ge(s_gm, 1)
            A(gmat[:, :, :].rearrange("p a b -> p (a b)"), PS[:, 3, :], ACT.Copy, scale=1.0 / N).then_inc(s_gmc, 1)

            idx_pass(2, 0, TURNS)
            idx_pass(3, 0, TURNS)

            act.wait_ge(s_b1t, 1)
            A(fr["b1T"], PS[:, 0, 0:NE * HT], ACT.Copy).then_inc(s_b1c, 1)

            def ahead(q, step, par, n):
                if step == 1:
                    act.wait_ge(s_gt, q + 1)
                    A(fr["gT"][:, :, 0:n * P], PS[:, 0:2, 0:n * P], ACT.Copy).then_inc(s_gtc, 1)
                if step == 2:
                    act.wait_ge(s_h, q + 1)
                    A(fr["gT"].rearrange("p a b -> p (a b)")[:, 0:n * F],
                      fr["gr"].rearrange("p a b -> p (a b)")[:, 0:n * F], ACT.Relu).then_inc(s_rl, 1)
                if step == 3:
                    act.wait_ge(s_v1, q + 1)
                    A(sm["rstd"][:, 1, 0:n], sm["rstd"][:, 0, 0:n], ACT.Sqrt).then_inc(s_d1, 1)
                if step == 4:
                    act.wait_ge(s_v2, q + 1)
                    A(sm["rstd"][:, 1, 0:n], sm["rstd"][:, 0, 0:n], ACT.Sqrt).then_inc(s_d2, 1)
                if step == 5:
                    act.wait_ge(s_xft, q + 1)
                    A(xft[par][:, :, 0:n * P], PS[:, 0:2, 0:n * P], ACT.Copy).then_inc(s_xftc, 1)
                if step == 6:
                    act.wait_ge(s_e1, q + 1)
                    A(sm["wts"][:, 1, 0:n], sm["wts"][:, 0, 0:n], ACT.Exp).then_inc(s_ex, 1)

            def expert(q, e, par, n):
                for t in range(HT):
                    act.wait_ge(s_ph, q * (NE * HT) + (e * HT + t + 1))
                    act.wait_ge(s_py, q * (NE * HT) + (e * HT + t + 1))
                    A(fa_["ht"][:, t, 0:n * P], PS[:, 4 + t % 2, 0:n * P], ACT.Gelu,
                      bias=fr["b1T"][:, e * HT + t:e * HT + t + 1]).then_inc(s_ht, 1)

            last_stage(act, ahead, expert)

        @block.vector
        def _(dve):
            link = Chain(dve, s_dve)
            V = nc.vector
            TS, TT, STT = V.tensor_scalar, V.tensor_tensor, V.scalar_tensor_tensor

            def newton(s, v, r, s2):
                link(V.reciprocal(r, s))
                link(TT(r, v, r, ALU.mult))
                link(TT(s2, s, r, ALU.add))
                link(TS(s2, s2, 0.5, None, ALU.mult))
                link(V.reciprocal(r, s2))

            def keys(o):
                link(TS(ti[:, 0, :], edges[:, o, :], 7, None, ALU.logical_shift_right))
                link(V.tensor_copy(key16, ti[:, 0, :]))
                link(V.memset(pos, float(NO_CHUNK * P)))

            def count_block(o, b):
                link(TS(oh16[:, 0, :], key16, iota_f[:, ds(b, 1)], 0.0, ALU.is_equal, ALU.add, accum_out=rowtot[:, ds(b, 1)]))

            def first_places(o):
                V.memset(z16[:, 0:1], 0.0).then_inc(s_rowtot[o], 1)
                dve.wait_ge(s_rowtot[o], 1)
                dve.wait_ge(s_cnt[o], 1)
                before, total = PS[:, 3 + 4 * o, 0:NB], PS[:, 3 + 4 * o, 64:64 + NB]
                link(TS(nch_i[:, 0, :], total, float(P - 1), None, ALU.add))
                link(TS(nch_i[:, 1, :], nch_i[:, 0, :], 7, None, ALU.logical_shift_right))
                link(V.tensor_copy(nch[:, 0:NB], nch_i[:, 1, :]))
                link(V.tensor_tensor_scan(endc[:, 0:NB], nch[:, 0:NB], nch[:, 0:NB], 0.0, ALU.add, ALU.bypass))
                link(TT(base[:, 0:NB], endc[:, 0:NB], nch[:, 0:NB], ALU.subtract))
                link(TS(base[:, 0:NB], base[:, 0:NB], float(P), -1.0, ALU.mult, ALU.add))
                link(TT(base[:, 0:NB], base[:, 0:NB], before, ALU.add))
                link(V.memset(base[:, NB:SORT_TURNS], float(NO_CHUNK * P)))
                link(TT(ge[:, :, :], iota_w[:, :].unsqueeze(2).broadcast_to([P, NW, NB]),
                        endc[:, 0:NB].unsqueeze(1).broadcast_to([P, NW, NB]), ALU.is_ge))
                link(V.tensor_reduce(bw[:, :], ge[:, :, :], AX.X, ALU.add))
                TS(bw_i[:, :], bw[:, :], float(NB - 1), None, ALU.min).then_inc(s_bw[o], 1)

            def place_block(o, b, k, steps=(0, 1, 2)):
                if 0 in steps:
                    link(TS(oh16[:, k, :], key16, iota_f[:, ds(b, 1)], None, ALU.is_equal))
                if 1 in steps:
                    link(V.tensor_tensor_scan(run, oh16[:, k, :], oh16[:, k, :], base[:, ds(b, 1)], ALU.add, ALU.bypass))
                if 2 in steps:
                    settle(dve)
                    link(V.copy_predicated(pos, oh16[:, k, :].bitcast(u16), run))

            def fields(o):
                key, other = edges[:, o, :], edges[:, 1 - o, :]
                link(V.tensor_copy(ti[:, 0, :], pos))
                link(TS(ti[:, 1, :], ti[:, 0, :], 7, None, ALU.logical_shift_right))
                link(V.tensor_copy(chunk_of[o][:, 0:EC], ti[:, 1, :]))
                link(TS(ti[:, 1, :], ti[:, 0, :], P - 1, None, ALU.bitwise_and))
                link(V.tensor_copy(slot_of[o][:, 0:EC], ti[:, 1, :]))
                link(TS(ti[:, 0, :], other, 2, None, ALU.logical_shift_right))
                link(V.tensor_copy(field_a[o][:, 0:EC], ti[:, 0, :]))
                link(TS(ti[:, 0, :], other, 3, 8, ALU.bitwise_and, ALU.logical_shift_left))
                link(TS(ti[:, 1, :], key, P - 1, None, ALU.bitwise_and))
                if o:
                    for v in (chunk_of[o], slot_of[o], field_a[o], field_b[o]):
                        m = V.memset(v[:, EC:EL], 0.0)
                    link(m)
                STT(out=field_b[o][:, 0:EC], in0=ti[:, 1, :], scalar=1.0, in1=ti[:, 0, :], op0=ALU.add, op1=ALU.add).then_inc(s_ranked[o], 1)
                dve.wait_ge(s_ranked[o], 1)

            dve.wait_ge(s_edges, 64)
            dve.wait_ge(s_const, N_CONST)
            keys(0)
            with dve.Fori(0, NR7) as i:
                link.enter(i, R7)
                for k in range(R7):
                    count_block(0, i * R7 + k)
            link.leave(NR7)
            dve.wait_ge(s_x, 32)
            with dve.Fori(0, NR7) as i:
                link.enter(i, 3)
                for k in range(R7):
                    m = V.bn_stats(stats7[:, k, :], x_sb[:, ds(i * R7 + k, 1), :].rearrange("p a f -> p (a f)"))
                link(m)
                settle(dve)
                for k in range(R7):
                    m = V.bn_aggr(mv7[:, k, :], stats7[:, k, :])
                link(m)
                link(V.tensor_copy(ln["mv"][:, ds(i * R7, R7), :], mv7[:, :, :]))
            link.leave(NR7)
            TS(var_c[:, 0:NB], ln["mv"][:, :, 1], EPS, None, ALU.add).then_inc(s_stat, 1)
            dve.wait_ge(s_stat, 1)
            dve.wait_ge(s_sd, 1)
            newton(tmp_c[:, 0:NB], var_c[:, 0:NB], rstd_c[:, 0:NB], mean_c[:, 0:NB])
            STT(out=mean_c[:, 0:NB], in0=ln["mv"][:, :, 0], scalar=-1.0, in1=rstd_c[:, 0:NB], op0=ALU.mult, op1=ALU.mult).then_inc(s_ln, 1)

            def sort_column(o, i, k):
                c = i * U + k
                dve.wait_ge(s_used[o], i * U + (k + 1))
                TS(ohc[:, k % 4, :], iota_c[:, :], chunk_of[o][:, ds(c, 1)], None, ALU.is_equal)
                TS(ohs[:, k % 4, :], iota_h[:, :], slot_of[o][:, ds(c, 1)], None, ALU.is_equal).then_inc(s_oh[o], 1)

            def unpack(o):
                dve.wait_ge(s_sorted[o], 1)
                a, b = ti.rearrange("p a b -> p (a b)")[:, 0:NC], r["unp"]
                link(V.tensor_copy(a.rearrange("p (h c) -> p h c", h=2), PS[:, 0:2, 0:HC]))
                link(V.tensor_copy(b.rearrange("p (h c) -> p h c", h=2), PS[:, 2:4, 0:HC]))
                link(TS(idx[o][:, 0:NC], b, 255, None, ALU.bitwise_and))
                link(V.tensor_copy(dl[o][:, 0:NC], idx[o][:, 0:NC]))
                V.memset(idx[o][:, NC:NC + U], 0)
                link(V.memset(dl[o][:, NC:NC + U], 0.0))
                link(TS(a, a, 2, None, ALU.logical_shift_left))
                link(TS(b, b, 8, None, ALU.logical_shift_right))
                TT(idx[o][:, 0:NC], a, b, ALU.bitwise_or).then_inc(s_idx[o], 1)

            first_places(0)
            with dve.Fori(0, NR7) as i:
                link.enter(i, 3 * R7)
                for k in range(R7):
                    place_block(0, i * R7 + k, k % 2)
            link.leave(NR7)
            fields(0)
            dve.wait_ge(s_bwd[0], 16)
            keys(1)
            half = SORT_TURNS // 2
            with dve.Fori(0, half) as i:
                link.enter(i, 2)
                for k in range(U):
                    sort_column(0, i, k)
                    if k % 8 == 3:
                        count_block(1, i * 2 + k // 8)
            link.leave(half)
            first_places(1)
            with dve.Fori(half, SORT_TURNS) as i:
                j = i * 2 - 2 * half
                link.enter(i - half, 6)
                for k in range(U):
                    sort_column(0, i, k)
                    if k % 8 in (1, 3, 5):
                        place_block(1, j + k // 8, k // 8, (k % 8 // 2,))
            link.leave(SORT_TURNS - half)
            dve.wait_ge(s_xn, NB)
            dve.wait_ge(s_xpad, 16)
            fields(1)
            unpack(0)

            def block_numbers(p, i):
                return nc.values_load_multi_w_load_instructions(
                    blk_row[p % 2][0:1, ds(i * U, U)], engines=(DVE,), min_val=0, max_val=NB - 1,
                    skip_runtime_bounds_check_because="computed on the chip as a minimum with NB - 1")[1]

            def add_chunk(p, i, k, block_of):
                dve.wait_ge(s_mm[p], i * U + (U + k + 1))
                dve.wait_ge(s_acc[p], i * U + (k + AB))
                a = accs[p % 2][:, ds(block_of[k], 1), :].rearrange("p a f -> p (a f)")
                TT(a, a, PS[:, 4 + k % AB, 0:FC], ALU.add).then_inc(s_acc[p], 1)

            def one_hots(p, i, h):
                dve.wait_ge(s_mm[p], i * U + (8 * h + 8))
                TT(ohg[:, 8 * h:8 * h + 8, :], iota_1[:, :].unsqueeze(1).broadcast_to([P, 8, P]),
                   dl[p % 2][:, ds(i * U + 8 * h, 8)].unsqueeze(2).broadcast_to([P, 8, P]), ALU.is_equal).then_inc(s_ohg[p], 1)

            def acc_pass(p, start, end, body=None, links=0):
                if start == 0:
                    if p:
                        dve.wait_ge(s_ohg[p - 1], 2 * TURNS + 1)
                    one_hots(p, 0, 0)
                with dve.Fori(start, end) as i:
                    if links:
                        link.enter(i - start if start else i, links)
                    block_of = block_numbers(p, i)
                    for k in range(U):
                        if body is not None:
                            body(i, k)
                        if k == 3:
                            one_hots(p, i, 1)
                        if k == 11:
                            one_hots(p, i + 1, 0)
                        add_chunk(p, i, k, block_of)
                if links:
                    link.leave(end - start)

            def inverse(p):
                dve.wait_ge(s_acc[p], NC + AB)
                link(TS(inv[:, :], accs[p % 2][:, :, F], 1.0, None, ALU.max))
                link(V.reciprocal(inv[:, :], inv[:, :]))

            def scaled(p, n):
                a = accs[p % 2][:, n * R7:(n + 1) * R7, 0:F]
                return a, inv[:, n * R7:(n + 1) * R7].unsqueeze(2).broadcast_to([P, R7, F])

            def finish_mean(p):
                inverse(p)
                for n in range(NR7):
                    a, v = scaled(p, n)
                    TT(a, a, v, ALU.mult).then_inc(s_fin[p], 1)

            dve.wait_ge(s_bwr[0], 16)
            dve.wait_ge(s_bwr[1], 16)
            dve.wait_ge(s_zero[0], 2)
            for c in range(LEAD):
                sort_column(1, 0, c)
            acc_pass(0, 0, SORT_TURNS, lambda i, k: sort_column(1, i, k + LEAD))
            acc_pass(0, SORT_TURNS, TURNS)
            unpack(1)
            finish_mean(0)

            def kv_body(i, k):
                if k == 5:
                    dve.wait_ge(s_sq, i + 1)
                    link(V.tensor_reduce(mx["ss"][:, 0, :], mx["sq"], AX.X, ALU.add))
                    TS(mx["ss"][:, 0, :], mx["ss"][:, 0, :], 1.0 / DH, EPS, ALU.mult, ALU.add).then_inc(s_var, 1)
                if k == 11:
                    dve.wait_ge(s_sdv, i + 1)
                    newton(mx["ss"][:, 1, :], mx["ss"][:, 0, :], mx["ss"][:, 2, :], mx["ss"][:, 3, :])
                    TT(mx["kv"], PS[:, 0:2, :].rearrange("p a (h d) -> p (a h) d", d=DH),
                       mx["ss"][:, 2, :].unsqueeze(2).broadcast_to([P, 2 * HEADS, DH]), ALU.mult).then_inc(s_kn, 1)

            dve.wait_ge(s_zero[1], 1)
            acc_pass(1, 0, NB, kv_body, links=6)
            acc_pass(1, NB, TURNS)

            inverse(1)
            dve.wait_ge(s_dots, 1)
            for n in range(NR7):
                a, v = scaled(1, n)
                link(TT(a, a, v, ALU.mult))
                TT(a, a, vecs[:, 0, :].unsqueeze(1).broadcast_to([P, R7, F]), ALU.add).then_inc(s_hz, 1)
                dve.wait_ge(s_hz, n + 1)
                dve.wait_ge(s_hr, n + 1)
                link(TS(a, a, 0.0, a_col[:, 0:1], ALU.min, ALU.mult))
                TT(a, a, positive[n % 2], ALU.add).then_inc(s_fin[1], 1)
            V.memset(mx["dots"], 0.0).then_inc(s_dz, 1)

            def res_body(i, k):
                if k == 8:
                    dve.wait_ge(s_mix, i + 2)
                    dve.wait_ge(s_sl, i * 48 + 48)
                    link(TT(mx["rs"], mx["xb"], PS[:, 0, 0:F], ALU.add))
                    link(TT(mx["rs"], mx["rs"], vecs[:, 1, :], ALU.add))
                    TT(mx["sk"], mx["xnb"], vecs[:, 2, :], ALU.add).then_inc(s_res, 1)

            dve.wait_ge(s_zero[2], 1)
            acc_pass(2, 0, NB, res_body, links=2)
            acc_pass(2, NB, TURNS)
            finish_mean(2)
            dve.wait_ge(s_zero[3], 1)
            acc_pass(3, 0, TURNS)
            dve.wait_ge(s_acc[3], NC + AB)
            V.memset(z16[:, 0:1], 0.0).then_inc(s_fin[3], 1)
            dve.wait_ge(s_fin[3], 1)

            dve.wait_ge(s_fw, N_FW)

            def bc(v, n):
                return v.unsqueeze(1).broadcast_to([P, n, F])

            def norm(which, source, target, s_v, s_d, q, n):
                rstd, mv = sm["rstd"], sm["mv"]
                for j in range(n):
                    m = V.bn_stats(sm["stats"][:, j, :], source[:, j, :])
                link(m)
                settle(dve)
                for j in range(n):
                    m = V.bn_aggr(mv[:, which, j, :], sm["stats"][:, j, :])
                link(m)
                TS(rstd[:, 0, 0:n], mv[:, which, 0:n, 1], EPS, None, ALU.add).then_inc(s_v, 1)
                dve.wait_ge(s_v, q + 1)
                dve.wait_ge(s_d, q + 1)
                newton(rstd[:, 1, 0:n], rstd[:, 0, 0:n], rstd[:, 2, 0:n], rstd[:, 3, 0:n])
                for j in range(n):
                    m = TS(target[:, j, :], source[:, j, :], mv[:, which, j, 0:1], rstd[:, 2, j:j + 1],
                           ALU.subtract, ALU.mult)
                link(m)

            def ahead(q, step, par, n):
                gr, w = fr["gr"][:, 0:n, :], sm["wts"]
                x2 = fa_["x2"][:, par, :].rearrange("p (b f) -> p b f", f=F)[:, 0:n, :]
                tmp = fr["gT"].rearrange("p a b -> p (a b)")[:, 0:n * F].rearrange("p (b f) -> p b f", f=F)
                if step == 0:
                    a = accs[1][:, ds(q * G, n), :]
                    link(TS(sm["inv"][:, 0:n], a[:, :, F], 1.0, None, ALU.max))
                    link(V.reciprocal(sm["inv"][:, 0:n], sm["inv"][:, 0:n]))
                    TT(gr, a[:, :, 0:F], sm["inv"][:, 0:n].unsqueeze(2).broadcast_to([P, n, F]), ALU.mult).then_inc(s_gr, 1)
                if step == 2:
                    dve.wait_ge(s_u, q + 1)
                    dve.wait_ge(s_fl, q * 32 + 32)
                    TT(gr, fo["skip"][:, 0:n, :], PS[:, 2:4, :].rearrange("p a (b f) -> p (a b) f", f=F)[:, 0:n, :], ALU.add).then_inc(s_h, 1)
                    dve.wait_ge(s_h, q + 1)
                    dve.wait_ge(s_rl, q + 1)
                    link(TS(gr, gr, 0.0, a_col[:, 0:1], ALU.min, ALU.mult))
                    link(TT(gr, gr, tmp, ALU.add))
                    link(TT(x2, gr, fo["resid"][:, 0:n, :], ALU.add))

                if step == 3:
                    norm(0, x2, gr, s_v1, s_d1, q, n)
                if step == 4:
                    norm(1, gr, gr, s_v2, s_d2, q, n)
                    link(TT(gr, gr, bc(fr["gb"][:, 0, :], n), ALU.mult))
                    TT(gr, gr, bc(fr["gb"][:, 1, :], n), ALU.add).then_inc(s_xf, 1)
                if step == 6:
                    dve.wait_ge(s_lg, q + 1)
                    lg = sm["lg"][:, 0:n, :]
                    link(TT(lg, PS[:, 2, 0:n * NE].rearrange("p (b e) -> p b e", e=NE),
                            fr["br"].unsqueeze(1).broadcast_to([P, n, NE]), ALU.add))
                    settle(dve)
                    for j in range(n):
                        m = V.max(sm["top"][:, j, :], sm["lg"][:, j, :])
                    link(m)
                    settle(dve)
                    for j in range(n):
                        m = V.max_index(sm["topi"][:, j, :], sm["top"][:, j, :], sm["lg"][:, j, :])
                    link(m)
                    link(V.tensor_copy(sm["topf"][:, 0:n, :], sm["topi"][:, 0:n, :]))
                    TT(w[:, 0, 0:n], sm["top"][:, 0:n, 1], sm["top"][:, 0:n, 0], ALU.subtract).then_inc(s_e1, 1)
                    dve.wait_ge(s_ex, q + 1)
                    link(TS(w[:, 2, 0:n], w[:, 1, 0:n], 1.0, None, ALU.add))
                    link(V.reciprocal(w[:, 3, 0:n], w[:, 2, 0:n]))
                    link(TT(w[:, 4, 0:n], w[:, 3, 0:n], w[:, 1, 0:n], ALU.mult))
                    wf, oh = sm["wf"][:, par, 0:n, :], sm["oh"][:, 0:n, :]
                    io = iota_f[:, 0:NE].unsqueeze(1).broadcast_to([P, n, NE])

                    def b8(v):
                        return v.unsqueeze(2).broadcast_to([P, n, NE])
                    link(TT(wf, io, b8(sm["topf"][:, 0:n, 0]), ALU.is_equal))
                    link(TT(wf, wf, b8(w[:, 3, 0:n]), ALU.mult))
                    link(TT(oh, io, b8(sm["topf"][:, 0:n, 1]), ALU.is_equal))
                    link(TT(oh, oh, b8(w[:, 4, 0:n]), ALU.mult))
                    TT(wf, wf, oh, ALU.add).then_inc(s_wf, 1)
                if step == 7:
                    dve.wait_ge(s_wt, q + 1)
                    V.tensor_copy(sm["wT"][0:n * NE, :], PS[0:n * NE, 3, 0:P]).then_inc(s_wtc, 1)
                    dve.wait_ge(s_y0, q + 1)
                    dve.wait_ge(s_yfree, q + 1)
                    TT(fg["y"][:, par, 0:n * F].rearrange("p (b f) -> p b f", f=F), x2,
                       PS[:, 0:2, :].rearrange("p a (b f) -> p (a b) f", f=F)[:, 0:n, :], ALU.add).then_inc(s_y0c, 1)

            def expert(q, e, par, n):
                dve.wait_ge(s_py, q * (NE * HT) + (e * HT + HT + HT))
                if e == 0:
                    dve.wait_ge(s_y0c, q + 1)
                dve.wait_ge(s_pyc, q * NE + (e + 1))
                for j in range(n):
                    y = fg["y"][:, par, j * F:(j + 1) * F]
                    m = STT(out=y, in0=PS[:, 6 + j // 2, (j % 2) * F:(j % 2 + 1) * F],
                            scalar=sm["wf"][:, par, j, e:e + 1], in1=y, op0=ALU.mult, op1=ALU.add)
                m.then_inc(s_pyc, 1)

            last_stage(dve, ahead, expert, link, LINKS)

        @block.tensor
        def _(pe):
            MM, TR = nc.tensor.matmul, nc.tensor.transpose
            pe.wait_ge(s_const, N_CONST)
            pe.wait_ge(s_raw, 32)
            for kt in range(KT):
                for q in range(2 * PAIRS):
                    MM(PS[:, kt * 2 + q // PAIRS, (q % PAIRS) * P:(q % PAIRS + 1) * P],
                       raw["wkv"][:, q, kt * P:(kt + 1) * P], cen[:, :], start=True, stop=True)
            for q in range(PAIRS):
                for kt in range(KT):
                    m = TR(PS[:, 4 + q // 2, (q % 2) * F + kt * P:(q % 2) * F + (kt + 1) * P],
                           raw["wout"][:, kt, q * P:(q + 1) * P], ident[:, :])
            m.then_inc(s_wkv, 1)

            def count(o):
                pe.wait_ge(s_rowtot[o], 1)
                bank = 3 + 4 * o
                MM(PS[:, bank, 0:NB], lower[:, :], rowtot[:, 0:NB], start=True, stop=True)
                MM(PS[:, bank, 64:64 + NB], ones[:, :], rowtot[:, 0:NB], start=True, stop=True).then_inc(s_cnt[o], 1)

            pe.wait_ge(s_wkvc, 2)
            count(0)
            pe.wait_ge(s_w, 16)
            with pe.Fori(0, NR7) as i:
                for k in range(R7 + 1):
                    if k < R7:
                        pe.wait_ge(s_xn, i * R7 + (k + 1))
                        for kt in range(KT):
                            m = TR(PS[:, 4 + k % 2, kt * P:(kt + 1) * P], ln["xn"][:, k, kt * P:(kt + 1) * P], ident[:, :])
                        m.then_inc(s_xt, 1)
                    if k >= 1:
                        pe.wait_ge(s_xtc, i * R7 + k)
                        for kt in range(KT):
                            m = MM(PS[:, 6 + (k - 1) % 2, 0:F], ln["xt"][:, k - 1, kt * P:(kt + 1) * P],
                                   ln["w1"][:, kt, :], start=kt == 0, stop=kt == KT - 1)
                        m.then_inc(s_t1, 1)

            def open_sort(o):
                zero = [MM(PS[:, 2 * f + h, 0:HC], z16[:, :], iota_c[:, 0:HC], start=True, stop=False)
                        for f in range(2) for h in range(2)]
                for m in zero:
                    m.then_inc(s_used[o], 1)

            def sort_column(o, i, k):
                pe.wait_ge(s_ohs[o], i * U + (k + 1))
                for f in range(2):
                    for h in range(2):
                        m = MM(PS[:, 2 * f + h, 0:HC], ohv[:, k % 4, f, :], ohc[:, k % 4, h * HC:(h + 1) * HC],
                               start=False, stop=False)
                m.then_inc(s_used[o], 1)

            def close_sort(o):
                for f in range(2):
                    for h in range(2):
                        m = MM(PS[:, 2 * f + h, 0:HC], z16[:, :], iota_c[:, 0:HC], start=False, stop=True)
                m.then_inc(s_sorted[o], 1)

            pe.wait_ge(s_bw[0], 1)
            open_sort(0)
            half = SORT_TURNS // 2
            with pe.Fori(0, half) as i:
                for k in range(U):
                    sort_column(0, i, k)
            count(1)
            with pe.Fori(half, SORT_TURNS) as i:
                for k in range(U):
                    sort_column(0, i, k)
            close_sort(0)

            def product_pass(p, start, end, body=None):
                if start == 0:
                    pe.sem_inc(s_mm[p], U)
                    pe.sem_inc(s_acc[p], AB)
                with pe.Fori(start, end) as i:
                    for k in range(U):
                        if k % 8 == 0:
                            pe.wait_ge(s_ohg[p], i * 2 + (k // 8 + 1))
                        pe.wait_ge(s_g[k], (i + (p * TURNS + 1)) * 16)
                        pe.wait_ge(s_acc[p], i * U + (k + 1))
                        MM(PS[:, 4 + k % AB, 0:FC], ohg[:, k, :], gbuf[:, k, :], start=True, stop=True).then_inc(s_mm[p], 1)
                        if body is not None:
                            body(i, k)

            pe.wait_ge(s_idx[0], 1)
            open_sort(1)
            product_pass(0, 0, SORT_TURNS, lambda i, k: sort_column(1, i, k))
            close_sort(1)
            product_pass(0, SORT_TURNS, TURNS)

            def kv_body(i, k):
                if k == 1:
                    pe.wait_ge(s_xtl, i * 16 + 16)
                    pe.wait_ge(s_kn, i + 1)
                    for h in range(2):
                        for kt in range(KT):
                            m = MM(PS[:, h, :], mx["xt"][:, kt, :], mx["wkv"][:, kt, h * INNER:(h + 1) * INNER],
                                   start=kt == 0, stop=kt == KT - 1)
                    m.then_inc(s_kv, 1)
                if k == 15:
                    pe.wait_ge(s_kn, i + 2)
                    kv = mx["kv"].rearrange("p h d -> p (h d)")
                    for q in range(PAIRS):
                        MM(PS[:, 2, q * P:(q + 1) * P], kv[:, INNER + q * P:INNER + (q + 1) * P],
                           kv[:, q * P:(q + 1) * P], start=False, stop=False, skip_group_check=True)

            pe.wait_ge(s_idx[1], 1)
            pe.wait_ge(s_wl, 48)
            pe.sem_inc(s_kv, 1)
            pe.sem_inc(s_kn, 1)
            MM(PS[:, 2, :], z16[:, :], iota_c[:, 0:512], start=True, stop=False, skip_group_check=True)
            product_pass(1, 0, NB, kv_body)
            MM(PS[:, 2, :], z16[:, :], iota_c[:, 0:512], start=False, stop=True, skip_group_check=True).then_inc(s_dots, 1)
            product_pass(1, NB, TURNS)

            pe.wait_ge(s_dcp, 1)
            for q in range(PAIRS):
                m = MM(PS[:, q // 2, (q % 2) * F:(q % 2 + 1) * F], mx["dots"][:, q, :], mx["woutT"][:, q, :], start=True, stop=True)
            m.then_inc(s_pp, 1)
            pe.wait_ge(s_ppc, 1)
            for kt in range(KT):
                for q in range(PAIRS):
                    m = MM(PS[:, 3, kt * F:(kt + 1) * F], mx["wq"][:, q, kt * P:(kt + 1) * P], mx["pp"][:, q, :],
                           start=q == 0, stop=q == PAIRS - 1)
            m.then_inc(s_gm, 1)
            pe.wait_ge(s_gmc, 1)

            def mix_body(i, k):
                if k == 4:
                    pe.wait_ge(s_sl, i * 48 + 48)
                    pe.wait_ge(s_mix, i + 1)
                    pe.wait_ge(s_res, i + 1)
                    for kt in range(KT):
                        m = MM(PS[:, 0, 0:F], mx["xt"][:, kt, :], gmat[:, kt, :], start=kt == 0, stop=kt == KT - 1)
                    m.then_inc(s_mix, 1)

            pe.sem_inc(s_mix, 1)
            pe.sem_inc(s_res, 1)
            product_pass(2, 0, NB, mix_body)
            product_pass(2, NB, TURNS)
            product_pass(3, 0, TURNS)

            pe.wait_ge(s_fw, N_FW)
            TR(PS[:, 0, 0:NE * HT], fr["b1raw"][0:NE * HT, :], ident[0:NE * HT, 0:NE * HT]).then_inc(s_b1t, 1)
            pe.wait_ge(s_b1c, 1)
            pe.sem_inc(s_ht, 2)
            pe.sem_inc(s_py, HT)
            pe.sem_inc(s_pyc, 1)

            def ahead(q, step, par, n):
                if step == 1:
                    pe.wait_ge(s_gr, q + 1)
                    for j in range(n):
                        for kt in range(KT):
                            m = TR(PS[:, kt, j * P:(j + 1) * P], fr["gr"][:, j, kt * P:(kt + 1) * P], ident[:, :])
                    m.then_inc(s_gt, 1)
                if step == 2:
                    pe.wait_ge(s_gtc, q + 1)
                    for j in range(n):
                        for kt in range(KT):
                            m = MM(PS[:, 2 + j // 2, (j % 2) * F:(j % 2 + 1) * F], fr["gT"][:, kt, j * P:(j + 1) * P],
                                   fr["w2g"][:, kt, :], start=kt == 0, stop=kt == KT - 1)
                    m.then_inc(s_u, 1)
                if step == 5:
                    pe.wait_ge(s_xf, q + 1)
                    for j in range(n):
                        for kt in range(KT):
                            m = TR(PS[:, kt, j * P:(j + 1) * P], fr["gr"][:, j, kt * P:(kt + 1) * P], ident[:, :])
                    m.then_inc(s_xft, 1)
                if step == 6:
                    pe.wait_ge(s_xftc, q + 1)
                    for j in range(n):
                        for kt in range(KT):
                            m = MM(PS[:, 2, j * NE:(j + 1) * NE], xft[par][:, kt, j * P:(j + 1) * P],
                                   fr["wr"][:, kt, :], start=kt == 0, stop=kt == KT - 1)
                    m.then_inc(s_lg, 1)
                if step == 7:
                    pe.wait_ge(s_wf, q + 1)
                    TR(PS[0:n * NE, 3, 0:P], sm["wf"][:, par, 0:n, :].rearrange("p b e -> p (b e)"), ident[:, :]).then_inc(s_wt, 1)
                    pe.wait_ge(s_wtc, q + 1)
                    for j in range(n):
                        m = MM(PS[:, j // 2, (j % 2) * F:(j % 2 + 1) * F], sm["wT"][0:n * NE, :],
                               fr["b2e"][0:n * NE, j, :], start=True, stop=True)
                    m.then_inc(s_y0, 1)

            def expert(q, e, par, n):
                def down(t):
                    pe.wait_ge(s_ht, q * (NE * HT) + (e * HT + t + 1 + 2))
                    if t == 0:
                        pe.wait_ge(s_pyc, q * NE + (e + 1))
                    for j in range(n):
                        m = MM(PS[:, 6 + j // 2, (j % 2) * F:(j % 2 + 1) * F], fa_["ht"][:, t, j * P:(j + 1) * P],
                               fa_["w2"][:, e, t, :], start=t == 0 and j % 2 == 0, stop=t == HT - 1, skip_group_check=True)
                    m.then_inc(s_py, 1)

                for t in range(HT):
                    pe.wait_ge(s_ht, q * (NE * HT) + (e * HT + t + 1))
                    for kt in range(KT):
                        m = MM(PS[:, 4 + t % 2, 0:n * P], fr["w1"][:, e, kt, t * P:(t + 1) * P],
                               xft[par][:, kt, 0:n * P], start=kt == 0, stop=kt == KT - 1)
                    m.then_inc(s_ph, 1)
                    if t:
                        down(t - 1)
                down(HT - 1)

            last_stage(pe, ahead, expert)


_INS = ['x', 'src', 'dst', 'L0_gnn_W1', 'L0_gnn_b1', 'L0_gnn_W2', 'L0_gnn_b2', 'L0_gnn_a', 'L0_mix_Wqkv',
        'L0_mix_Wout', 'L0_mix_bout', 'L0_ffn_gamma', 'L0_ffn_beta', 'L0_ffn_Wr', 'L0_ffn_br', 'L0_ffn_W1',
        'L0_ffn_b1', 'L0_ffn_W2', 'L0_ffn_b2']


def kernel(**inputs):
    import numpy as np
    import concourse.bacc as bacc
    from concourse.bass_utils import run_bass_kernel_spmd

    nc = bacc.Bacc("TRN2", target_bir_lowering=False, num_devices=1)
    arrays, args = {}, []
    for name in _INS:
        a = np.ascontiguousarray(inputs[name])
        arrays[f"in_{name}"] = a
        args.append(nc.dram_tensor(f"in_{name}", a.shape, mybir.dt.from_np(a.dtype), kind="ExternalInput").ap())
    out = nc.dram_tensor("out_0", inputs['x'].shape, mybir.dt.float32, kind="ExternalOutput").ap()
    gps_layer(nc, *args, out)
    return run_bass_kernel_spmd(nc, [arrays], core_ids=[0]).results[0]["out_0"]
```

```python
import concourse.bass as bass
from concourse import mybir
from contextlib import ExitStack

P = 128


class Chain:

    def __init__(self, engine, semaphore):
        self.engine, self.semaphore, self.count, self.step = engine, semaphore, 0, None

    def __call__(self, instruction):
        self.mark(instruction)
        self.wait()

    def mark(self, instruction):
        instruction.then_inc(self.semaphore, 1)
        self.count += 1

    def wait(self, but=0):
        self.engine.wait_ge(self.semaphore, self.count - but if self.step is None else self.step + (self.count - but))

    def enter(self, i, per_turn):
        self.step, self.per_turn, self.at_entry = i * per_turn, per_turn, self.count

    def leave(self, turns):
        assert self.count - self.at_entry == self.per_turn, (self.count - self.at_entry, self.per_turn)
        self.count, self.step = self.at_entry + self.per_turn * turns, None


def gps_layer(nc, x, src, dst, gnn_w1, gnn_b1, gnn_w2, gnn_b2, gnn_a, wqkv, wout, bout,
              gamma, beta, wr, br, ffn_w1, ffn_b1, ffn_w2, ffn_b2, out):
    f32, i32, f16 = mybir.dt.float32, mybir.dt.int32, mybir.dt.float16
    u16, u32 = mybir.dt.uint16, mybir.dt.uint32
    ALU, ACT, AX = mybir.AluOpType, mybir.ActivationFunctionType, mybir.AxisListType
    DVE = mybir.EngineType.DVE
    ds = bass.ds
    N, F = x.shape
    E = src.shape[0]
    KT = F // P
    NB = -(-N // P)
    LAST = N - (NB - 1) * P
    COLS, REST = E // P, E % P
    U = 16
    EC = -(-(COLS + 1) // U) * U
    NC = -(-((E + NB * (P - 1)) // P) // U) * U
    HC = NC // 2
    NW = -(-NC // P)
    TURNS, SORT_TURNS = NC // U, EC // U
    SC_TURNS = 12
    SW = 64
    SC_FROM = 2 * SC_TURNS
    COUNT_END = SC_FROM + 7
    IB = 4
    FC = F + 1
    AB = 4
    LEAD = 3
    NO_CHUNK = 2048
    R7 = 7
    NR7 = NB // R7
    HEADS, DH = 8, 64
    INNER = HEADS * DH
    PAIRS = INNER // P
    EPS = 1e-5
    NE, D, H = ffn_w1.shape
    HT = H // P
    G = 4
    ER = 4
    NCE = -(-((2 * N + NE * (P - 1)) // P) // ER) * ER
    CE7 = 7
    NG = NB // G
    assert NB % R7 == 0 and NB == NG * G + 1 and NG % 2 == 0 and SORT_TURNS % 2 == 0 and HC <= 512
    assert NB < SORT_TURNS and NB < TURNS and SC_FROM * U <= COLS
    assert NB == 7 * (COUNT_END - SC_FROM) and NB <= 3 * (SORT_TURNS - COUNT_END) <= SW

    ctx = ExitStack()
    with ctx:
        def sb(name, shape, dt):
            return ctx.enter_context(nc.sbuf_tensor(name, shape, dt))

        def sem(name):
            return ctx.enter_context(nc.semaphore(name))

        def dram(name, shape, dt=f32):
            return nc.dram_tensor(name, shape, dt).ap()

        ctx.enter_context(nc.allow_non_contiguous_dma("the last column of edges"))
        PS = ctx.enter_context(nc.psum_tensor("PS", [P, 8, 512], f32))

        tables = [dram(f"table{p}", (NB * P, F)) for p in range(4)]
        blk_dram = [dram(f"blk_dram{o}", (P, NW), i32) for o in range(2)]
        xpad_d = dram("xpad_d", (NB * P, F))
        xn_d = dram("xn_d", (NB * P, F))
        xt_d = dram("xt_d", (NB * P, F))
        wkv_d = dram("wkv_d", (P, KT * 2 * INNER))
        wout_d = dram("wout_d", (P, PAIRS * F))
        resid_d = dram("resid_d", (NB * P, F))
        xf_d = dram("xf_d", (NB * P, F))
        ye_d = dram("ye_d", (2 * NB * P + NCE * P, F))
        scattered_d = dram("scattered_d", (P * NC, 1), i32)
        skip_d = dram("skip_d", (NB * P, F))

        accs = [sb(f"acc{n}", [P, NB, FC], f32) for n in range(2)]
        REGION = 13000
        region = sb("region", [P, REGION], f32)
        gbuf = sb("gbuf", [P, U, FC], f32)
        ohg = sb("ohg", [P, U, P], f32)
        idx = [sb(f"idx{o}", [P, NC + U], i32) for o in range(2)]
        dl = [sb(f"dl{o}", [P, NC + U], f16) for o in range(2)]
        blk_row = [sb(f"blk_row{o}", [1, P * NW], i32) for o in range(2)]
        idxb = sb("idxb", [P, U], i32)
        iota_c = sb("iota_c", [P, NC], f16)
        iota_f = sb("iota_f", [P, P], f32)
        iota_h = sb("iota_h", [P, P], f16)
        iota_1 = sb("iota_1", [P, P], f16)
        iota_w = sb("iota_w", [P, NW], f32)
        lower = sb("lower", [P, P], f32)
        ones = sb("ones", [P, P], f32)
        ident = sb("ident", [P, P], f32)
        cen = sb("cen", [P, P], f32)
        z16 = sb("z16", [P, P], f16)
        inv = sb("inv", [P, NB], f32)
        vecs = sb("vecs", [P, 3, F], f32)
        a_col = sb("a_col", [P, 1], f32)
        gmat = sb("gmat", [P, KT, F], f32)

        def carve(base, sizes):
            views, at = {}, 0
            for name, (shape, dt) in sizes.items():
                n = 1
                for s in shape:
                    n *= s
                words = -(-n * (2 if dt in (f16, u16) else 4) // 4)
                v = base[:, at:at + words]
                if dt is not f32:
                    v = v.bitcast(dt)
                if len(shape) == 2:
                    v = v.rearrange("p (a b) -> p a b", b=shape[1])
                if len(shape) == 3:
                    v = v.rearrange("p (a b c) -> p a b c", b=shape[1], c=shape[2])
                views[name] = v
                at += words
            assert at <= base.shape[1], (at, base.shape)
            return views

        acc_flat = [a[:, :, :].rearrange("p b f -> p (b f)") for a in accs]
        gbuf_flat = gbuf[:, :, :].rearrange("p b f -> p (b f)")
        ohg_flat = ohg[:, :, :].rearrange("p b f -> p (b f)")

        ge = carve(ohg_flat, {"ge": ((NW, NB), f32)})["ge"]
        scattered = ohg_flat[:, NW * NB:NW * NB + NC].bitcast(i32)
        r = carve(region, {
            "edges": ((2, EC), i32), "key16": ((EC,), f16), "oh16": ((2, EC), f16), "run": ((EC,), f32),
            "pos": ((EC,), f32), "ti": ((2, EC), i32), "chunk0": ((EC,), f32), "slot0": ((EC,), f32),
            "fa0": ((EC,), f32), "fb0": ((EC,), f32), "ohc": ((4, NC), f16), "ohs": ((4, P), f16),
            "ohv": ((8, P), f16), "unp": ((NC,), i32)})
        EL = EC + LEAD
        r1 = carve(acc_flat[1], {"chunk1": ((EL,), f32), "slot1": ((EL,), f32), "fa1": ((EL,), f32),
                                 "fb1": ((EL,), f32)})
        r.update(r1)
        edges, key16, oh16, run, pos, ti = (r[k] for k in ("edges", "key16", "oh16", "run", "pos", "ti"))
        chunk_of = [r["chunk0"], r["chunk1"]]
        slot_of = [r["slot0"], r["slot1"]]
        field_a = [r["fa0"], r["fa1"]]
        field_b = [r["fb0"], r["fb1"]]
        ohc, ohs, ohv = r["ohc"], r["ohs"], r["ohv"].rearrange("p (k f) n -> p k f n", f=2)
        small = sb("small", [P, 8, SW], f32)
        rowtot, nch, endc, base, mean_c, rstd_c, var_c, tmp_c = (small[:, k, :] for k in range(8))
        stats7, mv7 = sb("stats7", [P, R7, 6], f32), sb("mv7", [P, R7, 2], f32)
        nch_i = sb("nch_i", [P, 2, NB], i32)
        bw = sb("bw", [P, NW], f32)
        bw_i = sb("bw_i", [P, NW], i32)

        x_sb = acc_flat[1][:, 0:NB * F].rearrange("p (b f) -> p b f", f=F)
        ln = carve(acc_flat[0], {
            "xn": ((R7, F), f32), "xt": ((R7, F), f32), "t1": ((R7, F), f32), "mv": ((NB, 2), f32),
            "w1": ((KT, F), f32), "wkv": ((KT * 2 * INNER,), f32), "woutT": ((PAIRS * F,), f32),
            "place": ((SC_FROM * U,), i32), "edge": ((SC_FROM * U,), i32), "places": ((2, U), i32), "edges": ((2, U), i32)})
        mx = carve(region, {
            "wkv": ((KT, 2 * INNER), f32), "wq": ((PAIRS, F), f32), "woutT": ((PAIRS, F), f32),
            "sq": ((2 * HEADS, DH), f32), "kv": ((2 * HEADS, DH), f32), "xt": ((KT, P), f32),
            "dots": ((PAIRS, P), f32), "pp": ((PAIRS, F), f32), "ss": ((4, 2 * HEADS), f32),
            "xb": ((F,), f32), "xnb": ((F,), f32), "rs": ((F,), f32), "sk": ((F,), f32)})
        positive = [region[:, at:at + R7 * F].rearrange("p (b f) -> p b f", f=F)
                    for at in (0, KT * 2 * INNER + 2 * PAIRS * F)]
        raw = carve(gbuf_flat, {"wkv": ((2 * PAIRS, F), f32), "wout": ((KT, INNER), f32)})

        fr = carve(region, {"w1": ((NE, KT, H), f32), "b2r": ((NE, F), f32), "w2g": ((KT, F), f32),
                            "gb": ((2, F), f32), "gr": ((G, F), f32), "wr": ((KT, NE), f32), "br": ((NE,), f32)})
        fa_ = carve(acc_flat[0], {"w2": ((NE, HT, F), f32), "b1r": ((NE, H), f32)})
        fg = carve(gbuf_flat, {"gT": ((KT, G * P), f32), "xh": ((2, G * F), f32), "xft": ((KT, G * P), f32)})
        fo = carve(ohg_flat, {"skip": ((G, F), f32), "resid": ((G, F), f32)})
        xh = [fg["xh"][:, n, :].rearrange("p (b f) -> p b f", f=F) for n in range(2)]
        NK = 2 * NB
        fs = sb("fs", [P, 800], f32)
        sm = carve(fs, {"inv": ((G,), f32), "stats": ((G, 6), f32), "mv": ((G, 2), f32), "rstd": ((4, G), f32),
                        "lg": ((G, NE), f32), "top": ((G, 8), f32), "topi": ((G, 8), u32),
                        "tv": ((2, NB), f32), "key": ((2, NB), f32), "pad": ((1,), f32),
                        "tok": ((NCE + ER,), i32), "dest": ((NCE,), i32), "wgt": ((NCE,), f32),
                        "eid": ((NCE + ER,), i32), "tokb": ((ER,), i32), "destb": ((ER,), i32)})
        fb_ = carve(ohg_flat, {"pos": ((NK,), f32), "run": ((NK,), f32), "oh": ((NK,), f32), "chunk": ((NK,), f32),
                               "slot": ((NK,), f32), "ti": ((2, NK), i32), "val": ((NK,), f32), "w": ((4, NB), f32),
                               "wt": ((2, NB), f32), "cnt": ((NE,), f32), "nch": ((NE,), f32), "nchi": ((2, NE), i32),
                               "endc": ((NE,), f32), "base": ((NE,), f32)})
        fc = carve(gbuf_flat, {"ohs": ((CE7, P), f32), "ohc": ((CE7, NCE), f32), "ohv": ((CE7, 2, NCE), f32)})
        fd = carve(gbuf_flat, {"iw": ((NCE + ER,), f32), "ge": ((NCE + ER, NE), f32), "ew": ((NCE + ER,), f32),
                               "dummy": ((NCE,), f32), "none": ((NCE,), f32), "a": ((NCE,), f32)})
        fe = carve(gbuf_flat, {"xg": ((ER, F), f32), "h": ((2, H), f32), "hT": ((2, H), f32), "y": ((ER, F), f32)})
        xT = carve(ohg_flat, {"xT": ((2, F), f32)})["xT"]
        yl = [gbuf_flat[:, n * 2 * G * F:(n + 1) * 2 * G * F].rearrange("p (b j f) -> p b j f", b=G, j=2) for n in range(2)]

        s_pad, s_const, s_raw = sem("s_pad"), sem("s_const"), sem("s_raw")
        s_edges, s_x, s_w, s_vec = sem("s_edges"), sem("s_x"), sem("s_w"), sem("s_vec")
        s_dve, s_pool = sem("s_dve"), sem("s_pool")
        s_rowtot, s_cnt, s_bw = [[sem(f"{n}{o}") for o in range(2)] for n in ("s_rowtot", "s_cnt", "s_bw")]
        s_bwd, s_bwr = [[sem(f"{n}{o}") for o in range(2)] for n in ("s_bwd", "s_bwr")]
        s_oh, s_ohs, s_used, s_sorted, s_idx = [[sem(f"{n}{o}") for o in range(2)]
                                                for n in ("s_oh", "s_ohs", "s_used", "s_sorted", "s_idx")]
        s_stat, s_sd, s_ln, s_xn, s_xt, s_xtc, s_t1, s_t1c, s_lnd, s_lnfree, s_xpad = [
            sem(n) for n in ("s_stat", "s_sd", "s_ln", "s_xn", "s_xt", "s_xtc", "s_t1", "s_t1c", "s_lnd", "s_lnfree", "s_xpad")]
        s_g = [sem(f"s_g{k}") for k in range(U)]
        s_idxb, s_ohg, s_mm, s_acc = [
            [sem(f"{n}_{p}") for p in range(4)] for n in ("s_idxb", "s_ohg", "s_mm", "s_acc")]
        s_zero, s_fin, s_tab = sem("s_zero"), sem("s_fin"), sem("s_tab")
        s_empty, s_emptied, s_places, s_scattered = [sem(n) for n in ("s_empty", "s_emptied", "s_places", "s_scattered")]
        s_sc = [sem(f"s_sc{h}") for h in range(2)]
        s_hz, s_hr = sem("s_hz"), sem("s_hr")
        s_wkv, s_wkvc, s_xtl, s_kv, s_sq, s_var, s_sdv, s_kn, s_dots = [
            sem(n) for n in ("s_wkv", "s_wkvc", "s_xtl", "s_kv", "s_sq", "s_var", "s_sdv", "s_kn", "s_dots")]
        s_dz, s_dcp, s_pp, s_ppc, s_gm, s_gmc = [sem(n) for n in ("s_dz", "s_dcp", "s_pp", "s_ppc", "s_gm", "s_gmc")]
        s_sl, s_mix, s_res, s_st = [sem(n) for n in ("s_sl", "s_mix", "s_res", "s_st")]
        s_wd, s_wl, s_settled = [sem(n) for n in ("s_wd", "s_wl", "s_settled")]
        s_fw = sem("s_fw")
        (s_fl, s_gr, s_gt, s_gtc, s_u, s_v1, s_d1, s_v2, s_d2, s_xh, s_xf, s_xfd, s_xfree, s_xft, s_xftc, s_lg, s_lgc,
         s_ei, s_ed, s_ex, s_ecnt, s_etot, s_eoh, s_eohv, s_eused, s_eopen, s_esort, s_iw, s_ready,
         s_it, s_t1e, s_c1, s_up, s_b1, s_ge, s_t2, s_c2, s_dn, s_b2, s_scl, s_yfreed, s_add, s_od) = [sem(n) for n in (
             "s_fl s_gr s_gt s_gtc s_u s_v1 s_d1 s_v2 s_d2 s_xh s_xf s_xfd s_xfree s_xft s_xftc s_lg s_lgc "
             "s_ei s_ed s_ex s_ecnt s_etot s_eoh s_eohv s_eused s_eopen s_esort s_iw s_ready "
             "s_it s_t1e s_c1 s_up s_b1 s_ge s_t2 s_c2 s_dn s_b2 s_scl s_yfreed s_add s_od").split()]
        s_ys = [sem(f"s_ys{k}") for k in range(ER)]
        s_yl = [sem(f"s_yl{k}") for k in range(2)]
        sort_from = (SC_FROM, 0)
        N_CONST = 9
        XG0 = 4 * TURNS * 16
        N_VEC = 4 * 16
        N_FW = 9 * 16

        def rows(d, b, n=1):
            return d[ds(b * P, n * P), :].rearrange("(b p) f -> p b f", p=P)

        def by_group(engine, first, second, third, link=None, links=0):
            first(0, 0, G)
            first(1, 1, G)
            second(0, 0, G)
            with engine.Fori(0, (NG - 2) // 2) as i:
                if link is not None:
                    link.enter(i, links)
                for q, par in ((i * 2 + 1, 1), (i * 2 + 2, 0)):
                    first(q + 1, 1 - par, G)
                    second(q, par, G)
                    third(q - 1, 1 - par, G)
            if link is not None:
                link.leave((NG - 2) // 2)
            first(NG, 0, 1)
            second(NG - 1, 1, G)
            third(NG - 2, 0, G)
            second(NG, 0, 1)
            third(NG - 1, 1, G)
            third(NG, 0, 1)

        def settle(engine):
            engine.sem_inc(s_settled, 1)

        block = ctx.enter_context(nc.Block())

        @block.sync
        def _(sp):
            sp.wait_ge(s_pad, 2)
            for n, e in enumerate((dst, src)):
                sp.dma_start(edges[:, n, 0:COLS], e[0:COLS * P].rearrange("(p c) -> p c", p=P)).then_inc(s_edges, 16)
                sp.dma_start(edges[0:REST, n, COLS:COLS + 1],
                             e[COLS * P:E].rearrange("(p c) -> p c", c=1)).then_inc(s_edges, 16)
            sp.dma_start(x_sb[:, 0:NB - 1, :], rows(x, 0, NB - 1)).then_inc(s_x, 16)
            sp.dma_start(x_sb[0:LAST, NB - 1, :], x[(NB - 1) * P:N, :]).then_inc(s_x, 16)
            sp.dma_start(ln["w1"], gnn_w1.rearrange("(k p) f -> p k f", p=P)).then_inc(s_w, 16)
            for n, v in enumerate((gnn_b1, bout, gnn_b2)):
                sp.dma_start(vecs[:, n, :], v.unsqueeze(0).broadcast_to([P, F])).then_inc(s_vec, 16)
            sp.dma_start(a_col[:, :], gnn_a.unsqueeze(0).broadcast_to([P, 1])).then_inc(s_vec, 16)
            sp.wait_ge(s_x, 32)
            sp.dma_start(rows(xpad_d, 0, NB), x_sb).then_inc(s_xpad, 16)
            def chunk_blocks(o):
                sp.wait_ge(s_bw[o], 1)
                sp.dma_start(blk_dram[o], bw_i[:, :]).then_inc(s_bwd[o], 16)
                sp.wait_ge(s_bwd[o], 16)
                sp.dma_start(blk_row[o][:, :], blk_dram[o].rearrange("(a p) w -> a (p w)", a=1)).then_inc(s_bwr[o], 16)
            sp.wait_ge(s_empty, 1)
            sp.dma_start(scattered_d.rearrange("(p c) a -> p (c a)", c=NC), scattered).then_inc(s_emptied, 16)
            sp.sem_inc(s_lnfree, 1)
            sp.wait_ge(s_wkvc, 2)
            sp.dma_start(wkv_d, ln["wkv"]).then_inc(s_wd, 16)
            sp.dma_start(wout_d, ln["woutT"]).then_inc(s_wd, 16)
            with sp.Fori(0, NR7) as i:
                for k in range(R7):
                    b = i * R7 + k
                    sp.wait_ge(s_xn, i * R7 + (k + 1))
                    settle(sp)
                    sp.dma_start(xn_d[ds(b * P, P), :], ln["xn"][:, k, :]).then_inc(s_lnd, 16)
                    sp.wait_ge(s_xtc, i * R7 + (k + 1))
                    settle(sp)
                    sp.dma_start(xt_d[ds(b * P, P), :], ln["xt"][:, k, :]).then_inc(s_lnd, 16)
                    sp.wait_ge(s_t1c, i * R7 + (k + 1))
                    settle(sp)
                    sp.dma_start(tables[0][ds(b * P, P), :], ln["t1"][:, k, :]).then_inc(s_lnd, 16)
                sp.wait_ge(s_lnd, (i + 1) * (48 * R7))
                sp.sem_inc(s_lnfree, 1)
            chunk_blocks(0)
            chunk_blocks(1)
            for h in range(2):
                sp.wait_ge(s_sc[h], SC_TURNS * U * 16)
            sp.dma_start(scattered, scattered_d.rearrange("(p c) a -> p (c a)", c=NC)).then_inc(s_scattered, 16)

            def store_table(p):
                for n in range(NR7):
                    sp.wait_ge(s_fin, p * NR7 + n + 1)
                    sp.dma_start(rows(tables[p + 1], n * R7, R7), accs[p % 2][:, n * R7:(n + 1) * R7, 0:F]).then_inc(s_tab, 16)

            sp.wait_ge(s_idx[1], 1)
            sp.wait_ge(s_ohs[1], EC + LEAD)
            sp.wait_ge(s_wd, 32)
            sp.dma_start(mx["wkv"].rearrange("p a b -> p (a b)"), wkv_d).then_inc(s_wl, 16)
            sp.dma_start(mx["woutT"].rearrange("p a b -> p (a b)"), wout_d).then_inc(s_wl, 16)
            sp.dma_start(mx["wq"], wqkv[0:INNER, :].rearrange("(q p) c -> p q c", p=P)).then_inc(s_wl, 16)
            store_table(0)
            with sp.Fori(0, NB) as i:
                sp.wait_ge(s_kv, i + 1)
                settle(sp)
                sp.dma_start(mx["xt"], xt_d[ds(i * P, P), :].rearrange("p (k n) -> p k n", k=KT)).then_inc(s_xtl, 16)
            store_table(1)
            sp.wait_ge(s_gm, 1)
            with sp.Fori(0, NB) as i:
                sp.dma_start(mx["xt"], xt_d[ds(i * P, P), :].rearrange("p (k n) -> p k n", k=KT)).then_inc(s_sl, 16)
                sp.dma_start(mx["xb"], xpad_d[ds(i * P, P), :]).then_inc(s_sl, 16)
                sp.dma_start(mx["xnb"], xn_d[ds(i * P, P), :]).then_inc(s_sl, 16)
                sp.wait_ge(s_res, i + 2)
                settle(sp)
                sp.dma_start(resid_d[ds(i * P, P), :], mx["rs"]).then_inc(s_st, 16)
                sp.dma_start(skip_d[ds(i * P, P), :], mx["sk"]).then_inc(s_st, 16)
                sp.wait_ge(s_st, (i + 1) * 32)
                settle(sp)
            store_table(2)
            sp.dma_start(fr["w1"], ffn_w1.rearrange("e (k p) h -> p e k h", p=P)).then_inc(s_fw, 16)
            sp.dma_start(fr["w2g"], gnn_w2.rearrange("(k p) f -> p k f", p=P)).then_inc(s_fw, 16)
            sp.dma_start(fr["b2r"], ffn_b2.rearrange("(a e) f -> a e f", a=1).broadcast_to([P, NE, F])).then_inc(s_fw, 16)
            sp.dma_start(fr["wr"], wr.rearrange("(k p) e -> p k e", p=P)).then_inc(s_fw, 16)
            for n, v in enumerate((gamma, beta)):
                sp.dma_start(fr["gb"][:, n, :], v.unsqueeze(0).broadcast_to([P, F])).then_inc(s_fw, 16)
            sp.dma_start(fr["br"], br.unsqueeze(0).broadcast_to([P, NE])).then_inc(s_fw, 16)
            sp.wait_ge(s_tab, 48 * NR7)
            sp.dma_start(fa_["w2"], ffn_w2.rearrange("e (t p) f -> p e t f", p=P)).then_inc(s_fw, 16)
            sp.dma_start(fa_["b1r"], ffn_b1.rearrange("(a e) f -> a e f", a=1).broadcast_to([P, NE, H])).then_inc(s_fw, 16)

            def load(q, par, n):
                if not (isinstance(q, int) and q == 0):
                    sp.wait_ge(s_v1, q)
                    settle(sp)
                sp.dma_start(fo["skip"][:, 0:n, :], rows(skip_d, q * G, n)).then_inc(s_fl, 16)
                sp.dma_start(fo["resid"][:, 0:n, :], rows(resid_d, q * G, n)).then_inc(s_fl, 16)

            def store(q, par, n):
                sp.wait_ge(s_xf, q + 1)
                settle(sp)
                sp.dma_start(rows(xf_d, q * G, n), xh[par][:, 0:n, :]).then_inc(s_xfd, 16)
                sp.wait_ge(s_xfd, (q + 1) * 16)
                sp.sem_inc(s_xfree, 1)

            sp.sem_inc(s_xfree, 2)
            sp.wait_ge(s_fin, 3 * NR7 + 1)
            load(0, 0, G)
            by_group(sp, lambda q, par, n: None, lambda q, par, n: None if n < G else load(q + 1, 1 - par, G if (not isinstance(q, int) or q < NG - 1) else 1),
                     store)
            sp.sem_inc(s_yfreed, ER)
            with sp.Fori(0, NCE // ER) as i:
                for k in range(ER):
                    sp.wait_ge(s_ys[k], i * 16 + 16)
                    sp.sem_inc(s_yfreed, 1)
            for k in range(ER):
                sp.wait_ge(s_g[k], XG0 + 16 * (NCE // ER + 1))
            for q in range(NG + 1):
                n = G if q < NG else 1
                m = P if q < NG else LAST
                if q >= 2:
                    sp.wait_ge(s_add, q - 1)
                sp.dma_start(yl[q % 2][0:m, 0:n, :, :], ye_d[q * G * 2 * P:q * G * 2 * P + n * 2 * m, :].rearrange("(b p j) f -> p b j f", p=m, j=2)).then_inc(s_yl[q % 2], 16)
            sp.wait_ge(s_xpad, 16)

        @block.gpsimd
        def _(pool):
            link = Chain(pool, s_pool)
            gp = nc.gpsimd
            gp.memset(edges, NB * P).then_inc(s_pad, 1)
            gp.memset(x_sb[:, NB - 1, :], 0.0).then_inc(s_pad, 1)
            gp.memset(scattered, 0).then_inc(s_empty, 1)

            def iota(t, n, base, mult):
                return gp.iota(t, pattern=[[1, n]], base=base, channel_multiplier=mult, allow_small_or_imprecise_dtypes=True)

            iota(iota_f[:, :], P, 0, 0).then_inc(s_const, 1)
            iota(iota_h[:, :], P, 0, 0).then_inc(s_const, 1)
            iota(iota_1[:, :], P, 1, 0).then_inc(s_const, 1)
            iota(iota_c[:, :], NC, 0, 0).then_inc(s_const, 1)
            iota(iota_w[:, :], NW, 0, NW).then_inc(s_const, 1)
            gp.memset(ones[:, :], 1.0).then_inc(s_const, 1)
            gp.memset(z16[:, :], 0.0).then_inc(s_const, 1)
            link(gp.memset(lower[:, :], 1.0))
            link(gp.affine_select(out=lower[:, :], in_=lower[:, :], compare_op=ALU.is_gt, fill=0.0, base=0,
                                  pattern=[[1, P]], channel_multiplier=-1))
            link(gp.memset(ident[:, :], 0.0))
            gp.affine_select(out=ident[:, :], in_=ident[:, :], compare_op=ALU.not_equal, fill=1.0, base=0,
                             pattern=[[-1, P]], channel_multiplier=1).then_inc(s_const, 1)
            pool.wait_ge(s_const, 8)
            link(gp.tensor_copy(cen[:, :], ident[:, :]))
            for h in range(P // DH):
                q = cen[h * DH:(h + 1) * DH, h * DH:(h + 1) * DH]
                link(gp.tensor_scalar(q, q, -1.0 / DH, None, ALU.add))
            link(gp.memset(sm["pad"], 0.0))
            gp.affine_select(out=sm["pad"], in_=sm["pad"], compare_op=ALU.is_gt, fill=float(NE), base=LAST,
                             pattern=[[0, 1]], channel_multiplier=-1).then_inc(s_const, 1)

            def memset_acc(p):
                gp.memset(accs[p % 2][:, :, :], 0.0).then_inc(s_zero, 1)

            def gather_pass(p):
                with pool.Fori(0, TURNS) as i:
                    for k in range(U):
                        if k % IB == 0:
                            pool.wait_ge(s_idxb[p], i * (U // IB) + (k // IB + 1))
                        pool.wait_ge(s_mm[p], i * U + (k + 1))
                        settle(pool)
                        gp.indirect_dma_start(gbuf[:, k, 0:F], None, tables[p],
                                              bass.IndirectOffsetOnAxis(idxb[:, k:k + 1], 0)).then_inc(s_g[k], 16)

            def scatter(h, c):
                link(gp.tensor_copy(ln["places"][:, h, :], ln["place"][:, ds(c, U)]))
                link(gp.tensor_copy(ln["edges"][:, h, :], ln["edge"][:, ds(c, U)]))
                settle(pool)
                for k in range(U):
                    gp.indirect_dma_start(scattered_d, bass.IndirectOffsetOnAxis(ln["places"][:, h, k:k + 1], 0),
                                          ln["edges"][:, h, k:k + 1], None).then_inc(s_sc[h], 16)

            pool.wait_ge(s_emptied, 16)
            pool.wait_ge(s_places, 1)
            for h in range(2):
                scatter(h, h * U)
            with pool.Fori(1, SC_TURNS) as i:
                link.enter(i - 1, 4)
                for h in range(2):
                    pool.wait_ge(s_sc[h], i * (U * 16))
                    scatter(h, i * 2 * U + h * U)
            link.leave(SC_TURNS - 1)
            for h in range(2):
                pool.wait_ge(s_sc[h], SC_TURNS * U * 16)
            pool.wait_ge(s_lnfree, NR7 + 1)
            pool.wait_ge(s_wd, 32)
            memset_acc(0)
            pool.wait_ge(s_wkv, 1)
            gp.memset(gbuf[:, :, F:FC], 1.0).then_inc(s_zero, 1)
            gather_pass(0)
            pool.wait_ge(s_idx[1], 1)
            memset_acc(1)
            pool.wait_ge(s_tab, 16 * NR7)
            gather_pass(1)
            memset_acc(2)
            pool.wait_ge(s_tab, 32 * NR7)
            gather_pass(2)
            memset_acc(3)
            pool.wait_ge(s_tab, 48 * NR7)
            gather_pass(3)

            def scale_shift(q, par, n):
                pool.wait_ge(s_xh, q + 1)
                v = xh[par][:, 0:n, :]
                link(gp.tensor_tensor(v, v, fr["gb"][:, 0, :].unsqueeze(1).broadcast_to([P, n, F]), ALU.mult))
                gp.tensor_tensor(v, v, fr["gb"][:, 1, :].unsqueeze(1).broadcast_to([P, n, F]), ALU.add).then_inc(s_xf, 1)

            def nothing(q, par, n):
                pass
            pool.wait_ge(s_fw, N_FW)
            by_group(pool, nothing, scale_shift, nothing, link, 2)

            pool.wait_ge(s_ei, 1)
            gp.iota(fb_["val"], pattern=[[1, 2], [2 * P, NB]], base=1, channel_multiplier=2,
                    allow_small_or_imprecise_dtypes=True).then_inc(s_ei, 1)
            with pool.Fori(0, NK // CE7) as i:
                pool.wait_ge(s_eoh, i + 1)
                for f, v in enumerate((fb_["val"], fb_["wt"].rearrange("p j b -> p (j b)"))):
                    if f == 0:
                        gp.tensor_tensor(fc["ohv"][:, :, 0, :], fc["ohc"], v[:, ds(i * CE7, CE7)].unsqueeze(2).broadcast_to([P, CE7, NCE]), ALU.mult).then_inc(s_eohv, 1)
            pool.wait_ge(s_esort, 1)
            gp.iota(fd["iw"], pattern=[[1, NCE + ER]], base=0, channel_multiplier=0, allow_small_or_imprecise_dtypes=True).then_inc(s_iw, 1)
            gp.iota(fd["dummy"], pattern=[[P, NCE]], base=2 * NB * P + 1, channel_multiplier=1, allow_small_or_imprecise_dtypes=True).then_inc(s_iw, 1)

            def gather(k, count):
                pool.wait_ge(s_it, count)
                settle(pool)
                gp.indirect_dma_start(fe["xg"][:, k, :], None, xf_d, bass.IndirectOffsetOnAxis(sm["tokb"][:, k:k + 1], 0)).then_inc(s_g[k], 16)

            pool.wait_ge(s_ready, 1)
            pool.wait_ge(s_xfree, 2 + NG + 1)
            for k in range(ER):
                gather(k, k + 1)
            with pool.Fori(0, NCE // ER) as i:
                for k in range(ER):
                    gather(k, i * ER + (ER + k + 1))
                    pool.wait_ge(s_scl, i * ER + (k + 1))
                    settle(pool)
                    gp.indirect_dma_start(ye_d, bass.IndirectOffsetOnAxis(sm["destb"][:, k:k + 1], 0), fe["y"][:, k, :], None).then_inc(s_ys[k], 16)

        @block.scalar
        def _(act):
            A = nc.scalar.activation
            act.dma_start(raw["wkv"], wqkv[INNER:3 * INNER, :].rearrange("(q p) c -> p q c", p=P)).then_inc(s_raw, 16)
            act.dma_start(raw["wout"], wout.rearrange("(k p) h -> p k h", p=P)).then_inc(s_raw, 16)
            act.wait_ge(s_wkv, 1)
            A(ln["wkv"], PS[:, 0:4, :].rearrange("p a b -> p (a b)"), ACT.Copy).then_inc(s_wkvc, 1)
            A(ln["woutT"], PS[:, 4:6, :].rearrange("p a b -> p (a b)"), ACT.Copy).then_inc(s_wkvc, 1)
            act.wait_ge(s_stat, 1)
            act.activation(tmp_c[:, 0:NB], var_c[:, 0:NB], ACT.Sqrt).then_inc(s_sd, 1)
            act.wait_ge(s_ln, 1)
            with act.Fori(0, NR7) as i:
                act.wait_ge(s_lnfree, i + 1)
                for k in range(R7 + 2):
                    if k < R7:
                        b = i * R7 + k
                        A(ln["xn"][:, k, :], x_sb[:, ds(b, 1), :].rearrange("p a f -> p (a f)"), ACT.Identity,
                          bias=mean_c[:, ds(b, 1)], scale=rstd_c[:, ds(b, 1)]).then_inc(s_xn, 1)
                    if 1 <= k <= R7:
                        act.wait_ge(s_xt, i * R7 + k)
                        A(ln["xt"][:, k - 1, :], PS[:, 4 + (k - 1) % 2, 0:F], ACT.Copy).then_inc(s_xtc, 1)
                    if k >= 2:
                        act.wait_ge(s_t1, i * R7 + (k - 1))
                        A(ln["t1"][:, k - 2, :], PS[:, 6 + (k - 2) % 2, 0:F], ACT.Copy).then_inc(s_t1c, 1)

            def sort_column(o, i, k):
                c = i * U + k
                act.wait_ge(s_oh[o], (i - sort_from[o]) * U + (k + 1))
                A(ohv[:, k % 4, 0, :], ohs[:, k % 4, :], ACT.Copy, scale=field_a[o][:, ds(c, 1)])
                A(ohv[:, k % 4, 1, :], ohs[:, k % 4, :], ACT.Copy, scale=field_b[o][:, ds(c, 1)]).then_inc(s_ohs[o], 1)

            with act.Fori(SC_FROM, SORT_TURNS) as i:
                for k in range(U):
                    sort_column(0, i, k)

            def row_numbers(p, i, h):
                act.wait_ge(s_mm[p], i * U + (IB * h + IB))
                nc.scalar.copy(idxb[:, IB * h:IB * h + IB], idx[p % 2][:, ds(i * U + IB * h, IB)]).then_inc(s_idxb[p], 1)

            def idx_pass(p, start, end, body=None):
                if start == 0:
                    if p:
                        act.wait_ge(s_idxb[p - 1], (U // IB) * TURNS + 1)
                    row_numbers(p, 0, 0)
                with act.Fori(start, end) as i:
                    for k in range(U):
                        if k < U // IB - 1:
                            row_numbers(p, i, k + 1)
                        if k == IB:
                            row_numbers(p, i + 1, 0)
                        if body is not None:
                            body(i, k)

            act.wait_ge(s_idx[0], 1)
            for c in range(LEAD):
                sort_column(1, 0, c)
            idx_pass(0, 0, SORT_TURNS, lambda i, k: sort_column(1, i, k + LEAD))
            idx_pass(0, SORT_TURNS, TURNS)

            act.wait_ge(s_fin, NR7)

            def with_kv(i, k):
                if k == 7:
                    act.wait_ge(s_kv, i + 2)
                    A(mx["sq"].rearrange("p h d -> p (h d)"), PS[:, 0:2, :].rearrange("p a b -> p (a b)"), ACT.Square).then_inc(s_sq, 1)
                if k == 10:
                    act.wait_ge(s_var, i + 1)
                    A(mx["ss"][:, 1, :], mx["ss"][:, 0, :], ACT.Sqrt).then_inc(s_sdv, 1)
            idx_pass(1, 0, NB, with_kv)
            idx_pass(1, NB, TURNS)
            for n in range(NR7):
                act.wait_ge(s_hz, n + 1)
                A(positive[n % 2], accs[1][:, n * R7:(n + 1) * R7, 0:F], ACT.Relu).then_inc(s_hr, 1)
            act.wait_ge(s_dz, 1)
            act.wait_ge(s_dots, 1)
            for q in range(PAIRS):
                for h in range(P // DH):
                    s = slice(h * DH, (h + 1) * DH)
                    m = A(mx["dots"][s, q, s], PS[s, 2, q * P + h * DH:q * P + (h + 1) * DH], ACT.Copy)
            m.then_inc(s_dcp, 1)
            act.wait_ge(s_pp, 1)
            A(mx["pp"].rearrange("p a b -> p (a b)"), PS[:, 0:2, :].rearrange("p a b -> p (a b)"), ACT.Copy).then_inc(s_ppc, 1)
            act.wait_ge(s_gm, 1)
            A(gmat[:, :, :].rearrange("p a b -> p (a b)"), PS[:, 3, :], ACT.Copy, scale=1.0 / N).then_inc(s_gmc, 1)

            idx_pass(2, 0, TURNS)
            idx_pass(3, 0, TURNS)

            def act_first(q, par, n):
                act.wait_ge(s_gt, q + 1)
                A(fg["gT"][:, :, 0:n * P], PS[:, 0:2, 0:n * P], ACT.Copy).then_inc(s_gtc, 1)

            def act_second(q, par, n):
                for s_v, s_d in ((s_v1, s_d1), (s_v2, s_d2)):
                    act.wait_ge(s_v, q + 1)
                    A(sm["rstd"][:, 1, 0:n], sm["rstd"][:, 0, 0:n], ACT.Sqrt).then_inc(s_d, 1)

            def act_third(q, par, n):
                act.wait_ge(s_xft, q + 1)
                A(fg["xft"][:, :, 0:n * P], PS[:, 6:8, 0:n * P], ACT.Copy).then_inc(s_xftc, 1)

            by_group(act, act_first, act_second, act_third)
            act.wait_ge(s_ed, 1)
            A(fb_["w"][:, 1, :], fb_["w"][:, 0, :], ACT.Exp).then_inc(s_ex, 1)

            def copy_x(k, count):
                act.wait_ge(s_t1e, count)
                A(xT[:, k % 2, :], PS[:, k % 2, 0:F], ACT.Copy).then_inc(s_c1, 1)

            def gelu(k, count):
                act.wait_ge(s_b1, count)
                A(fe["h"][:, k % 2, :], fe["h"][:, k % 2, :], ACT.Gelu).then_inc(s_ge, 1)

            act.wait_ge(s_ready, 1)
            copy_x(0, 1)
            gelu(0, 1)
            copy_x(1, 2)
            with act.Fori(0, NCE // ER) as i:
                for k in range(ER):
                    act.wait_ge(s_t2, i * ER + (k + 1))
                    A(fe["hT"][:, k % 2, :], PS[:, 4 + k % 2, :], ACT.Copy).then_inc(s_c2, 1)
                    copy_x(k, i * ER + (k + 3))
                    gelu(k + 1, i * ER + (k + 2))
                    act.wait_ge(s_b2, i * ER + (k + 3))
                    A(fe["y"][:, k, :], fe["y"][:, k, :], ACT.Copy, scale=sm["wgt"][:, ds(i * ER + k, 1)]).then_inc(s_scl, 1)

            for q in range(NG + 1):
                act.wait_ge(s_add, q + 1)
                if q < NG:
                    act.dma_start(rows(out, q * G, G), accs[1][:, q * G:(q + 1) * G, 0:F]).then_inc(s_od, 16)
                else:
                    act.dma_start(out[q * G * P:N, :], accs[1][0:LAST, q * G, 0:F]).then_inc(s_od, 16)
            act.wait_ge(s_od, 16 * (NG + 1))

        @block.vector
        def _(dve):
            link = Chain(dve, s_dve)
            V = nc.vector
            TS, TT, STT = V.tensor_scalar, V.tensor_tensor, V.scalar_tensor_tensor

            def newton(s, v, r, s2, steps=range(5)):
                for step in steps:
                    link.wait()
                    if step == 0:
                        link.mark(V.reciprocal(r, s))
                    if step == 1:
                        link.mark(TT(r, v, r, ALU.mult))
                    if step == 2:
                        link.mark(TT(s2, s, r, ALU.add))
                    if step == 3:
                        link.mark(TS(s2, s2, 0.5, None, ALU.mult))
                    if step == 4:
                        link.mark(V.reciprocal(r, s2))

            def keys(o):
                link(TS(ti[:, 0, :], edges[:, o, :], 7, None, ALU.logical_shift_right))
                link(V.tensor_copy(key16, ti[:, 0, :]))
                link(V.memset(pos, float(NO_CHUNK * P)))

            def count_block(o, b):
                link.wait()
                link.mark(TS(oh16[:, 0, :], key16, iota_f[:, ds(b, 1)], 0.0, ALU.is_equal, ALU.add, accum_out=rowtot[:, ds(b, 1)]))

            def first_places(o):
                link.wait()
                V.memset(z16[:, 0:1], 0.0).then_inc(s_rowtot[o], 1)
                dve.wait_ge(s_rowtot[o], 1)
                dve.wait_ge(s_cnt[o], 1)
                before, total = PS[:, 3 + 4 * o, 0:NB], PS[:, 3 + 4 * o, 64:64 + NB]
                link(TS(nch_i[:, 0, :], total, float(P - 1), None, ALU.add))
                link(TS(nch_i[:, 1, :], nch_i[:, 0, :], 7, None, ALU.logical_shift_right))
                link(V.tensor_copy(nch[:, 0:NB], nch_i[:, 1, :]))
                link(V.tensor_tensor_scan(endc[:, 0:NB], nch[:, 0:NB], nch[:, 0:NB], 0.0, ALU.add, ALU.bypass))
                link(TT(base[:, 0:NB], endc[:, 0:NB], nch[:, 0:NB], ALU.subtract))
                link(TS(base[:, 0:NB], base[:, 0:NB], float(P), -1.0, ALU.mult, ALU.add))
                link(TT(base[:, 0:NB], base[:, 0:NB], before, ALU.add))
                link(V.memset(base[:, NB:SW], float(NO_CHUNK * P)))
                link(TT(ge, iota_w[:, :].unsqueeze(2).broadcast_to([P, NW, NB]),
                        endc[:, 0:NB].unsqueeze(1).broadcast_to([P, NW, NB]), ALU.is_ge))
                link(V.tensor_reduce(bw[:, :], ge, AX.X, ALU.add))
                TS(bw_i[:, :], bw[:, :], float(NB - 1), None, ALU.min).then_inc(s_bw[o], 1)

            def place_block(o, b, k, steps=(0, 1, 2)):
                for step in steps:
                    link.wait()
                    if step == 0:
                        link.mark(TS(oh16[:, k, :], key16, iota_f[:, ds(b, 1)], None, ALU.is_equal))
                    if step == 1:
                        link.mark(V.tensor_tensor_scan(run, oh16[:, k, :], oh16[:, k, :], base[:, ds(b, 1)], ALU.add, ALU.bypass))
                    if step == 2:
                        settle(dve)
                        link.mark(V.copy_predicated(pos, oh16[:, k, :].bitcast(u16), run))

            def fields(o):
                key, other = edges[:, o, :], edges[:, 1 - o, :]
                link.wait()
                link(V.tensor_copy(ti[:, 0, :], pos))
                link(TS(ti[:, 1, :], ti[:, 0, :], 7, None, ALU.logical_shift_right))
                link(V.tensor_copy(chunk_of[o][:, 0:EC], ti[:, 1, :]))
                link(TS(ti[:, 1, :], ti[:, 0, :], P - 1, None, ALU.bitwise_and))
                link(V.tensor_copy(slot_of[o][:, 0:EC], ti[:, 1, :]))
                link(TS(ti[:, 0, :], other, 2, None, ALU.logical_shift_right))
                link(V.tensor_copy(field_a[o][:, 0:EC], ti[:, 0, :]))
                link(TS(ti[:, 0, :], other, 3, 8, ALU.bitwise_and, ALU.logical_shift_left))
                link(TS(ti[:, 1, :], key, P - 1, None, ALU.bitwise_and))
                if o:
                    for v in (chunk_of[o], slot_of[o], field_a[o], field_b[o]):
                        m = V.memset(v[:, EC:EL], 0.0)
                    link(m)
                link(STT(out=field_b[o][:, 0:EC], in0=ti[:, 1, :], scalar=1.0, in1=ti[:, 0, :], op0=ALU.add, op1=ALU.add))

            dve.wait_ge(s_edges, 64)
            dve.wait_ge(s_const, N_CONST)
            keys(0)
            with dve.Fori(0, NR7) as i:
                link.enter(i, R7)
                for k in range(R7):
                    count_block(0, i * R7 + k)
            link.leave(NR7)
            dve.wait_ge(s_x, 32)
            with dve.Fori(0, NR7) as i:
                link.enter(i, 3)
                for k in range(R7):
                    m = V.bn_stats(stats7[:, k, :], x_sb[:, ds(i * R7 + k, 1), :].rearrange("p a f -> p (a f)"))
                link(m)
                settle(dve)
                for k in range(R7):
                    m = V.bn_aggr(mv7[:, k, :], stats7[:, k, :])
                link(m)
                link(V.tensor_copy(ln["mv"][:, ds(i * R7, R7), :], mv7[:, :, :]))
            link.leave(NR7)
            TS(var_c[:, 0:NB], ln["mv"][:, :, 1], EPS, None, ALU.add).then_inc(s_stat, 1)
            dve.wait_ge(s_stat, 1)
            dve.wait_ge(s_sd, 1)
            newton(tmp_c[:, 0:NB], var_c[:, 0:NB], rstd_c[:, 0:NB], mean_c[:, 0:NB])
            link.wait()
            STT(out=mean_c[:, 0:NB], in0=ln["mv"][:, :, 0], scalar=-1.0, in1=rstd_c[:, 0:NB], op0=ALU.mult, op1=ALU.mult).then_inc(s_ln, 1)

            def sort_column(o, i, k):
                c = i * U + k
                dve.wait_ge(s_used[o], (i - sort_from[o]) * U + (k + 1))
                TS(ohc[:, k % 4, :], iota_c[:, :], chunk_of[o][:, ds(c, 1)], None, ALU.is_equal)
                TS(ohs[:, k % 4, :], iota_h[:, :], slot_of[o][:, ds(c, 1)], None, ALU.is_equal).then_inc(s_oh[o], 1)

            def unpack(o):
                dve.wait_ge(s_sorted[o], 1)
                a, b = ti.rearrange("p a b -> p (a b)")[:, 0:NC], r["unp"]
                link(V.tensor_copy(a.rearrange("p (h c) -> p h c", h=2), PS[:, 0:2, 0:HC]))
                link(V.tensor_copy(b.rearrange("p (h c) -> p h c", h=2), PS[:, 2:4, 0:HC]))
                if o == 0:
                    dve.wait_ge(s_scattered, 16)
                    t = idx[o][:, 0:NC]
                    link(TS(t, scattered, 1023, None, ALU.bitwise_and))
                    link(TT(b, b, t, ALU.bitwise_or))
                    link(TS(scattered, scattered, 10, None, ALU.logical_shift_right))
                    link(TT(a, a, scattered, ALU.bitwise_or))
                link(TS(idx[o][:, 0:NC], b, 255, None, ALU.bitwise_and))
                link(V.tensor_copy(dl[o][:, 0:NC], idx[o][:, 0:NC]))
                V.memset(idx[o][:, NC:NC + U], 0)
                link(V.memset(dl[o][:, NC:NC + U], 0.0))
                link(TS(a, a, 2, None, ALU.logical_shift_left))
                link(TS(b, b, 8, None, ALU.logical_shift_right))
                TT(idx[o][:, 0:NC], a, b, ALU.bitwise_or).then_inc(s_idx[o], 1)

            first_places(0)
            with dve.Fori(0, NR7) as i:
                link.enter(i, 3 * R7)
                place_block(0, i * R7, 0, (0,))
                for k in range(R7):
                    place_block(0, i * R7 + k, k % 2, (1,))
                    if k + 1 < R7:
                        link.mark(TS(oh16[:, (k + 1) % 2, :], key16, iota_f[:, ds(i * R7 + (k + 1), 1)], None, ALU.is_equal))
                    link.wait(1 if k + 1 < R7 else 0)
                    settle(dve)
                    link.mark(V.copy_predicated(pos, oh16[:, k % 2, :].bitcast(u16), run))
            link.leave(NR7)
            fields(0)
            c = slice(0, SC_FROM * U)
            link(STT(out=ln["place"], in0=slot_of[0][:, c], scalar=float(NC), in1=chunk_of[0][:, c], op0=ALU.mult, op1=ALU.add))
            STT(out=ln["edge"], in0=field_a[0][:, c], scalar=1024.0, in1=field_b[0][:, c], op0=ALU.mult, op1=ALU.add).then_inc(s_places, 1)
            dve.wait_ge(s_bwd[0], 16)
            keys(1)
            with dve.Fori(SC_FROM, COUNT_END) as i:
                link.enter(i - SC_FROM, 7)
                for k in range(U):
                    sort_column(0, i, k)
                    if k % 2 and k < 14:
                        count_block(1, (i - SC_FROM) * 7 + k // 2)
            link.leave(COUNT_END - SC_FROM)
            first_places(1)
            with dve.Fori(COUNT_END, SORT_TURNS) as i:
                j = i * 3 - 3 * COUNT_END
                link.enter(i - COUNT_END, 9)
                for k in range(U):
                    sort_column(0, i, k)
                    if k < 15:
                        place_block(1, j + k // 5, k // 5 % 2, (k % 5 // 2,) if k % 5 % 2 == 0 else ())
            link.leave(SORT_TURNS - COUNT_END)
            dve.wait_ge(s_xn, NB)
            dve.wait_ge(s_xpad, 16)
            fields(1)
            unpack(0)

            def block_numbers(p, i):
                return nc.values_load_multi_w_load_instructions(
                    blk_row[p % 2][0:1, ds(i * U, U)], engines=(DVE,), min_val=0, max_val=NB - 1,
                    skip_runtime_bounds_check_because="computed on the chip as a minimum with NB - 1")[1]

            def add_chunk(p, i, k, block_of):
                dve.wait_ge(s_mm[p], i * U + (U + k + 1))
                dve.wait_ge(s_acc[p], i * U + (k + AB))
                a = accs[p % 2][:, ds(block_of[k], 1), :].rearrange("p a f -> p (a f)")
                TT(a, a, PS[:, 4 + k % AB, 0:FC], ALU.add).then_inc(s_acc[p], 1)

            def one_hots(p, i, h):
                dve.wait_ge(s_mm[p], i * U + (8 * h + 8))
                TT(ohg[:, 8 * h:8 * h + 8, :], iota_1[:, :].unsqueeze(1).broadcast_to([P, 8, P]),
                   dl[p % 2][:, ds(i * U + 8 * h, 8)].unsqueeze(2).broadcast_to([P, 8, P]), ALU.is_equal).then_inc(s_ohg[p], 1)

            def acc_pass(p, start, end, body=None, links=0):
                if start == 0:
                    if p:
                        dve.wait_ge(s_ohg[p - 1], 2 * TURNS + 1)
                    one_hots(p, 0, 0)
                with dve.Fori(start, end) as i:
                    if links:
                        link.enter(i - start if start else i, links)
                    block_of = block_numbers(p, i)
                    for k in range(U):
                        if body is not None:
                            body(i, k)
                        if k == 1:
                            one_hots(p, i, 1)
                        if k == 9:
                            one_hots(p, i + 1, 0)
                        add_chunk(p, i, k, block_of)
                if links:
                    link.leave(end - start)

            def inverse(p):
                dve.wait_ge(s_acc[p], NC + AB)
                link(TS(inv[:, :], accs[p % 2][:, :, F], 1.0, None, ALU.max))
                link(V.reciprocal(inv[:, :], inv[:, :]))

            def scaled(p, n):
                a = accs[p % 2][:, n * R7:(n + 1) * R7, 0:F]
                return a, inv[:, n * R7:(n + 1) * R7].unsqueeze(2).broadcast_to([P, R7, F])

            def finish_mean(p):
                inverse(p)
                for n in range(NR7):
                    a, v = scaled(p, n)
                    TT(a, a, v, ALU.mult).then_inc(s_fin, 1)

            dve.wait_ge(s_bwr[0], 16)
            dve.wait_ge(s_bwr[1], 16)
            dve.wait_ge(s_zero, 2)
            for c in range(LEAD):
                sort_column(1, 0, c)
            acc_pass(0, 0, SORT_TURNS, lambda i, k: sort_column(1, i, k + LEAD))
            acc_pass(0, SORT_TURNS, TURNS)
            unpack(1)
            finish_mean(0)

            def kv_body(i, k):
                ss = [mx["ss"][:, n, :] for n in range(4)]
                if k == 8:
                    dve.wait_ge(s_sq, i + 1)
                    link(V.tensor_reduce(ss[0], mx["sq"], AX.X, ALU.add))
                    TS(ss[0], ss[0], 1.0 / DH, EPS, ALU.mult, ALU.add).then_inc(s_var, 1)
                if k == 10:
                    dve.wait_ge(s_var, i + 1)
                    dve.wait_ge(s_sdv, i + 1)
                if 10 <= k < 15:
                    newton(ss[1], ss[0], ss[2], ss[3], (k - 10,))
                if k == 15:
                    link.wait()
                    TT(mx["kv"], PS[:, 0:2, :].rearrange("p a (h d) -> p (a h) d", d=DH),
                       ss[2].unsqueeze(2).broadcast_to([P, 2 * HEADS, DH]), ALU.mult).then_inc(s_kn, 1)

            V.memset(mx["kv"], 0.0).then_inc(s_kn, 1)
            dve.wait_ge(s_zero, 3)
            acc_pass(1, 0, NB, kv_body, links=6)
            acc_pass(1, NB, TURNS)

            inverse(1)
            dve.wait_ge(s_vec, N_VEC)
            dve.wait_ge(s_dots, 1)
            for n in range(NR7):
                a, v = scaled(1, n)
                link(TT(a, a, v, ALU.mult))
                TT(a, a, vecs[:, 0, :].unsqueeze(1).broadcast_to([P, R7, F]), ALU.add).then_inc(s_hz, 1)
                dve.wait_ge(s_hz, n + 1)
                dve.wait_ge(s_hr, n + 1)
                link(TS(a, a, 0.0, a_col[:, 0:1], ALU.min, ALU.mult))
                TT(a, a, positive[n % 2], ALU.add).then_inc(s_fin, 1)
            V.memset(mx["dots"], 0.0).then_inc(s_dz, 1)

            def res_body(i, k):
                if k == 8:
                    dve.wait_ge(s_mix, i + 2)
                    dve.wait_ge(s_sl, i * 48 + 48)
                    link(TT(mx["rs"], mx["xb"], PS[:, 0, 0:F], ALU.add))
                    link(TT(mx["rs"], mx["rs"], vecs[:, 1, :], ALU.add))
                    TT(mx["sk"], mx["xnb"], vecs[:, 2, :], ALU.add).then_inc(s_res, 1)

            dve.wait_ge(s_zero, 4)
            acc_pass(2, 0, NB, res_body, links=2)
            acc_pass(2, NB, TURNS)
            finish_mean(2)
            dve.wait_ge(s_zero, 5)
            acc_pass(3, 0, TURNS)
            dve.wait_ge(s_acc[3], NC + AB)
            V.memset(z16[:, 0:1], 0.0).then_inc(s_fin, 1)
            dve.wait_ge(s_fin, 3 * NR7 + 1)

            dve.wait_ge(s_fw, N_FW)

            def blocks(q, n):
                return accs[1][:, ds(q * G, n), 0:F]

            def dve_first(q, par, n):
                if not (isinstance(q, int) and q == 0):
                    dve.wait_ge(s_gt, q)
                link(TS(sm["inv"][:, 0:n].unsqueeze(2), accs[1][:, ds(q * G, n), F:FC], 1.0, None, ALU.max))
                link(V.reciprocal(sm["inv"][:, 0:n], sm["inv"][:, 0:n]))
                TT(fr["gr"][:, 0:n, :], blocks(q, n), sm["inv"][:, 0:n].unsqueeze(2).broadcast_to([P, n, F]), ALU.mult).then_inc(s_gr, 1)

            def norm(source, target, s_v, s_d, q, n):
                rstd, mv = sm["rstd"], sm["mv"]
                settle(dve)
                for j in range(n):
                    m = V.bn_stats(sm["stats"][:, j, :], source(j))
                link(m)
                settle(dve)
                for j in range(n):
                    m = V.bn_aggr(mv[:, j, :], sm["stats"][:, j, :])
                link(m)
                TS(rstd[:, 0, 0:n], mv[:, 0:n, 1], EPS, None, ALU.add).then_inc(s_v, 1)
                dve.wait_ge(s_v, q + 1)
                dve.wait_ge(s_d, q + 1)
                newton(rstd[:, 1, 0:n], rstd[:, 0, 0:n], rstd[:, 2, 0:n], rstd[:, 3, 0:n])
                link.wait()
                for j in range(n):
                    m = TS(target(j), source(j), mv[:, j, 0:1], rstd[:, 2, j:j + 1], ALU.subtract, ALU.mult)
                return m

            def dve_second(q, par, n):
                x2, low = blocks(q, n), xh[par][:, 0:n, :]
                dve.wait_ge(s_u, q + 1)
                dve.wait_ge(s_fl, q * 32 + 32)
                dve.wait_ge(s_xfree, q + 1)
                link(TT(x2, fo["skip"][:, 0:n, :], PS[:, 2 + 2 * par:4 + 2 * par, :].rearrange("p a (b f) -> p (a b) f", f=F)[:, 0:n, :], ALU.add))
                link(TS(low, x2, 0.0, a_col[:, 0:1], ALU.min, ALU.mult))
                link(STT(out=x2, in0=x2, scalar=0.0, in1=fo["resid"][:, 0:n, :], op0=ALU.max, op1=ALU.add))
                link(TT(x2, x2, low, ALU.add))
                link(norm(lambda j: accs[1][:, ds(q * G + j, 1), 0:F].rearrange("p a f -> p (a f)"), lambda j: low[:, j, :], s_v1, s_d1, q, n))
                norm(lambda j: low[:, j, :], lambda j: low[:, j, :], s_v2, s_d2, q, n).then_inc(s_xh, 1)

            def dve_third(q, par, n):
                dve.wait_ge(s_lg, q + 1)
                link(TT(sm["lg"][:, 0:n, :], PS[:, 6, 0:n * NE].rearrange("p (b e) -> p b e", e=NE),
                        fr["br"].unsqueeze(1).broadcast_to([P, n, NE]), ALU.add))
                settle(dve)
                for j in range(n):
                    m = V.max(sm["top"][:, j, :], sm["lg"][:, j, :])
                link(m)
                settle(dve)
                for j in range(n):
                    m = V.max_index(sm["topi"][:, j, :], sm["top"][:, j, :], sm["lg"][:, j, :])
                link(m)
                V.tensor_copy(sm["tv"][:, :, ds(q * G, n)], sm["top"][:, 0:n, 0:2].rearrange("p b j -> p j b"))
                V.tensor_copy(sm["key"][:, :, ds(q * G, n)], sm["topi"][:, 0:n, 0:2].rearrange("p b j -> p j b")).then_inc(s_lgc, 1)

            by_group(dve, dve_first, dve_second, dve_third, link, 2 * (2 + 4 + 15 + 3))

            dve.wait_ge(s_lgc, 1 + NG + 1)
            w, wt, key = fb_["w"], fb_["wt"], sm["key"].rearrange("p j b -> p (j b)")
            TT(w[:, 0, :], sm["tv"][:, 1, :], sm["tv"][:, 0, :], ALU.subtract).then_inc(s_ed, 1)
            V.memset(fb_["run"], 0.0).then_inc(s_ei, 1)
            for j in range(2):
                link(TT(sm["key"][:, j, NB - 1:NB], sm["key"][:, j, NB - 1:NB], sm["pad"], ALU.add))
            for e in range(NE):
                link(TS(fb_["oh"], key, float(e), 0.0, ALU.is_equal, ALU.add, accum_out=fb_["cnt"][:, e:e + 1]))
            V.memset(fb_["pos"], float(NO_CHUNK * P)).then_inc(s_ecnt, 1)
            dve.wait_ge(s_ex, 1)
            link(TS(w[:, 2, :], w[:, 1, :], 1.0, None, ALU.add))
            link(V.reciprocal(wt[:, 0, :], w[:, 2, :]))
            link(TT(wt[:, 1, :], wt[:, 0, :], w[:, 1, :], ALU.mult))
            dve.wait_ge(s_etot, 1)
            dve.wait_ge(s_ecnt, 1)
            nci, nch_e, end_e, base_e = fb_["nchi"], fb_["nch"], fb_["endc"], fb_["base"]
            link(TS(nci[:, 0, :], PS[:, 0, 64:64 + NE], float(P - 1), None, ALU.add))
            link(TS(nci[:, 1, :], nci[:, 0, :], 7, None, ALU.logical_shift_right))
            link(V.tensor_copy(nch_e, nci[:, 1, :]))
            link(V.tensor_tensor_scan(end_e, nch_e, nch_e, 0.0, ALU.add, ALU.bypass))
            link(TT(base_e, end_e, nch_e, ALU.subtract))
            link(TS(base_e, base_e, float(P), -1.0, ALU.mult, ALU.add))
            link(TT(base_e, base_e, PS[:, 0, 0:NE], ALU.add))
            for e in range(NE):
                link(TS(fb_["oh"], key, float(e), None, ALU.is_equal))
                link(V.tensor_tensor_scan(fb_["run"], fb_["oh"], fb_["oh"], base_e[:, e:e + 1], ALU.add, ALU.bypass))
                link(V.copy_predicated(fb_["pos"], fb_["oh"].bitcast(i32), fb_["run"]))
            t = fb_["ti"]
            link(V.tensor_copy(t[:, 0, :], fb_["pos"]))
            link(TS(t[:, 1, :], t[:, 0, :], 7, None, ALU.logical_shift_right))
            link(V.tensor_copy(fb_["chunk"], t[:, 1, :]))
            link(TS(t[:, 1, :], t[:, 0, :], P - 1, None, ALU.bitwise_and))
            link(V.tensor_copy(fb_["slot"], t[:, 1, :]))
            dve.wait_ge(s_ei, 2)
            dve.wait_ge(s_xfree, 2 + NG + 1)
            with dve.Fori(0, NK // CE7) as i:
                dve.wait_ge(s_eused, i + 1)
                c = ds(i * CE7, CE7)

                def wide(v, n):
                    return v[:, c].unsqueeze(2).broadcast_to([P, CE7, n])
                TT(fc["ohc"], iota_c[:, 0:NCE].unsqueeze(1).broadcast_to([P, CE7, NCE]), wide(fb_["chunk"], NCE), ALU.is_equal).then_inc(s_eoh, 1)
                TT(fc["ohs"], iota_f[:, :].unsqueeze(1).broadcast_to([P, CE7, P]), wide(fb_["slot"], P), ALU.is_equal)
                dve.wait_ge(s_eoh, i + 1)
                TT(fc["ohv"][:, :, 1, :], fc["ohc"], wide(wt.rearrange("p j b -> p (j b)"), NCE), ALU.mult).then_inc(s_eopen, 1)
            dve.wait_ge(s_esort, 1)
            dve.wait_ge(s_iw, 2)
            v = PS[:, 0, 0:NCE]
            link(TS(fd["none"], v, 0.0, None, ALU.is_equal))
            link(V.memset(sm["tok"], 0))
            link(STT(out=fd["a"], in0=v, scalar=-1.0, in1=fd["none"], op0=ALU.add, op1=ALU.add))
            link(V.tensor_copy(sm["dest"], fd["a"]))
            link(TS(sm["tok"][:, 0:NCE], sm["dest"], 1, None, ALU.logical_shift_right))
            link(TT(fd["dummy"], fd["dummy"], fd["none"], ALU.mult))
            link(STT(out=sm["dest"], in0=v, scalar=-1.0, in1=fd["dummy"], op0=ALU.add, op1=ALU.add))
            link(V.tensor_copy(sm["wgt"], PS[:, 0, NCE:2 * NCE]))
            link(TT(fd["ge"], fd["iw"].unsqueeze(2).broadcast_to([P, NCE + ER, NE]),
                    end_e.unsqueeze(1).broadcast_to([P, NCE + ER, NE]), ALU.is_ge))
            link(V.tensor_reduce(fd["ew"], fd["ge"], AX.X, ALU.add))
            TS(sm["eid"], fd["ew"], float(NE - 1), None, ALU.min).then_inc(s_ready, 1)
            dve.wait_ge(s_ready, 1)

            def experts_of(i):
                return nc.values_load_multi_w_load_instructions(
                    sm["eid"][0:1, ds(i * ER, ER + 1)], engines=(DVE,), min_val=0, max_val=NE - 1,
                    skip_runtime_bounds_check_because="computed on the chip as a minimum with NE - 1")[1]

            def token_numbers(k, w):
                V.tensor_copy(sm["tokb"][:, k:k + 1], sm["tok"][:, ds(w, 1)]).then_inc(s_it, 1)

            def add_b1(k, count, e):
                dve.wait_ge(s_up, count)
                TT(fe["h"][:, k % 2, :], PS[:, 2 + k % 2, :], fa_["b1r"][:, ds(e, 1), :].rearrange("p a f -> p (a f)"), ALU.add).then_inc(s_b1, 1)

            for k in range(ER):
                token_numbers(k, k)
            e0 = nc.values_load_multi_w_load_instructions(
                sm["eid"][0:1, 0:1], engines=(DVE,), min_val=0, max_val=NE - 1,
                skip_runtime_bounds_check_because="computed on the chip as a minimum with NE - 1")[1][0]
            add_b1(0, 1, e0)
            with dve.Fori(0, NCE // ER) as i:
                es = experts_of(i)
                for k in range(ER):
                    w_ = i * ER + k
                    dve.wait_ge(s_t1e, w_ + 1)
                    token_numbers(k, w_ + ER)
                    add_b1(k + 1, w_ + 2, es[k + 1])
                    dve.wait_ge(s_yfreed, w_ + 1)
                    V.tensor_copy(sm["destb"][:, k:k + 1], sm["dest"][:, ds(w_, 1)])
                    dve.wait_ge(s_dn, w_ + 1)
                    TT(fe["y"][:, k, :], PS[:, 6 + k % 2, 0:F], fr["b2r"][:, ds(es[k], 1), :].rearrange("p a f -> p (a f)"), ALU.add).then_inc(s_b2, 1)

            for q in range(NG + 1):
                n, m = (G, P) if q < NG else (1, LAST)
                dve.wait_ge(s_yl[q % 2], 16 * (q // 2 + 1))
                x2 = accs[1][0:m, q * G:q * G + n, 0:F]
                link(TT(x2, x2, yl[q % 2][0:m, 0:n, 0, :], ALU.add))
                TT(x2, x2, yl[q % 2][0:m, 0:n, 1, :], ALU.add).then_inc(s_add, 1)

        @block.tensor
        def _(pe):
            MM, TR = nc.tensor.matmul, nc.tensor.transpose
            pe.wait_ge(s_const, N_CONST)
            pe.wait_ge(s_raw, 32)
            for kt in range(KT):
                for q in range(2 * PAIRS):
                    MM(PS[:, kt * 2 + q // PAIRS, (q % PAIRS) * P:(q % PAIRS + 1) * P],
                       raw["wkv"][:, q, kt * P:(kt + 1) * P], cen[:, :], start=True, stop=True)
            for q in range(PAIRS):
                for kt in range(KT):
                    m = TR(PS[:, 4 + q // 2, (q % 2) * F + kt * P:(q % 2) * F + (kt + 1) * P],
                           raw["wout"][:, kt, q * P:(q + 1) * P], ident[:, :])
            m.then_inc(s_wkv, 1)

            def count(o):
                pe.wait_ge(s_rowtot[o], 1)
                bank = 3 + 4 * o
                MM(PS[:, bank, 0:NB], lower[:, :], rowtot[:, 0:NB], start=True, stop=True)
                MM(PS[:, bank, 64:64 + NB], ones[:, :], rowtot[:, 0:NB], start=True, stop=True).then_inc(s_cnt[o], 1)

            pe.wait_ge(s_wkvc, 2)
            count(0)
            pe.wait_ge(s_w, 16)
            with pe.Fori(0, NR7) as i:
                for k in range(R7 + 1):
                    if k < R7:
                        pe.wait_ge(s_xn, i * R7 + (k + 1))
                        for kt in range(KT):
                            m = TR(PS[:, 4 + k % 2, kt * P:(kt + 1) * P], ln["xn"][:, k, kt * P:(kt + 1) * P], ident[:, :])
                        m.then_inc(s_xt, 1)
                    if k >= 1:
                        pe.wait_ge(s_xtc, i * R7 + k)
                        for kt in range(KT):
                            m = MM(PS[:, 6 + (k - 1) % 2, 0:F], ln["xt"][:, k - 1, kt * P:(kt + 1) * P],
                                   ln["w1"][:, kt, :], start=kt == 0, stop=kt == KT - 1)
                        m.then_inc(s_t1, 1)

            def open_sort(o):
                zero = [MM(PS[:, 2 * f + h, 0:HC], z16[:, :], iota_c[:, 0:HC], start=True, stop=False)
                        for f in range(2) for h in range(2)]
                for m in zero:
                    m.then_inc(s_used[o], 1)

            def sort_column(o, i, k):
                pe.wait_ge(s_ohs[o], (i - sort_from[o]) * U + (k + 1))
                for f in range(2):
                    for h in range(2):
                        m = MM(PS[:, 2 * f + h, 0:HC], ohv[:, k % 4, f, :], ohc[:, k % 4, h * HC:(h + 1) * HC],
                               start=False, stop=False)
                m.then_inc(s_used[o], 1)

            def close_sort(o):
                for f in range(2):
                    for h in range(2):
                        m = MM(PS[:, 2 * f + h, 0:HC], z16[:, :], iota_c[:, 0:HC], start=False, stop=True)
                m.then_inc(s_sorted[o], 1)

            pe.wait_ge(s_bw[0], 1)
            open_sort(0)
            with pe.Fori(SC_FROM, COUNT_END) as i:
                for k in range(U):
                    sort_column(0, i, k)
            count(1)
            with pe.Fori(COUNT_END, SORT_TURNS) as i:
                for k in range(U):
                    sort_column(0, i, k)
            close_sort(0)

            def product_pass(p, start, end, body=None):
                if start == 0:
                    pe.sem_inc(s_mm[p], U)
                    pe.sem_inc(s_acc[p], AB)
                with pe.Fori(start, end) as i:
                    for k in range(U):
                        if k % 8 == 0:
                            pe.wait_ge(s_ohg[p], i * 2 + (k // 8 + 1))
                        pe.wait_ge(s_g[k], (i + (p * TURNS + 1)) * 16)
                        pe.wait_ge(s_acc[p], i * U + (k + 1))
                        MM(PS[:, 4 + k % AB, 0:FC], ohg[:, k, :], gbuf[:, k, :], start=True, stop=True).then_inc(s_mm[p], 1)
                        if body is not None:
                            body(i, k)

            pe.wait_ge(s_idx[0], 1)
            open_sort(1)
            product_pass(0, 0, SORT_TURNS, lambda i, k: sort_column(1, i, k))
            close_sort(1)
            product_pass(0, SORT_TURNS, TURNS)

            def dots():
                kv = mx["kv"].rearrange("p h d -> p (h d)")
                for q in range(PAIRS):
                    MM(PS[:, 2, q * P:(q + 1) * P], kv[:, INNER + q * P:INNER + (q + 1) * P],
                       kv[:, q * P:(q + 1) * P], start=False, stop=False, skip_group_check=True)

            def kv_body(i, k):
                if k in (3, 5):
                    h = (k - 3) // 2
                    if h == 0:
                        pe.wait_ge(s_xtl, i * 16 + 16)
                        pe.wait_ge(s_kn, i + 1)
                    for kt in range(KT):
                        m = MM(PS[:, h, :], mx["xt"][:, kt, :], mx["wkv"][:, kt, h * INNER:(h + 1) * INNER],
                               start=kt == 0, stop=kt == KT - 1)
                    if h == 1:
                        m.then_inc(s_kv, 1)
                if k == 9:
                    dots()

            pe.wait_ge(s_idx[1], 1)
            pe.wait_ge(s_wl, 48)
            pe.sem_inc(s_kv, 1)
            MM(PS[:, 2, :], z16[:, :], iota_c[:, 0:512], start=True, stop=False, skip_group_check=True)
            product_pass(1, 0, NB, kv_body)
            pe.wait_ge(s_kn, NB + 1)
            dots()
            MM(PS[:, 2, :], z16[:, :], iota_c[:, 0:512], start=False, stop=True, skip_group_check=True).then_inc(s_dots, 1)
            product_pass(1, NB, TURNS)

            pe.wait_ge(s_dcp, 1)
            for q in range(PAIRS):
                m = MM(PS[:, q // 2, (q % 2) * F:(q % 2 + 1) * F], mx["dots"][:, q, :], mx["woutT"][:, q, :], start=True, stop=True)
            m.then_inc(s_pp, 1)
            pe.wait_ge(s_ppc, 1)
            for kt in range(KT):
                for q in range(PAIRS):
                    m = MM(PS[:, 3, kt * F:(kt + 1) * F], mx["wq"][:, q, kt * P:(kt + 1) * P], mx["pp"][:, q, :],
                           start=q == 0, stop=q == PAIRS - 1)
            m.then_inc(s_gm, 1)
            pe.wait_ge(s_gmc, 1)

            def mix_body(i, k):
                if k == 4:
                    pe.wait_ge(s_sl, i * 48 + 48)
                    pe.wait_ge(s_mix, i + 1)
                    pe.wait_ge(s_res, i + 1)
                    for kt in range(KT):
                        m = MM(PS[:, 0, 0:F], mx["xt"][:, kt, :], gmat[:, kt, :], start=kt == 0, stop=kt == KT - 1)
                    m.then_inc(s_mix, 1)

            pe.sem_inc(s_mix, 1)
            pe.sem_inc(s_res, 1)
            product_pass(2, 0, NB, mix_body)
            product_pass(2, NB, TURNS)
            product_pass(3, 0, TURNS)

            pe.wait_ge(s_fw, N_FW)
            pe.sem_inc(s_lgc, 1)

            def transposed(bank, source, n):
                for j in range(n):
                    for kt in range(KT):
                        m = TR(PS[:, bank + kt, j * P:(j + 1) * P], source[:, j, kt * P:(kt + 1) * P], ident[:, :])
                return m

            def pe_first(q, par, n):
                pe.wait_ge(s_gr, q + 1)
                transposed(0, fr["gr"], n).then_inc(s_gt, 1)
                pe.wait_ge(s_gtc, q + 1)
                for j in range(n):
                    for kt in range(KT):
                        m = MM(PS[:, 2 + 2 * par + j // 2, (j % 2) * F:(j % 2 + 1) * F], fg["gT"][:, kt, j * P:(j + 1) * P],
                               fr["w2g"][:, kt, :], start=kt == 0, stop=kt == KT - 1)
                m.then_inc(s_u, 1)

            def pe_second(q, par, n):
                pass

            def pe_third(q, par, n):
                pe.wait_ge(s_xf, q + 1)
                pe.wait_ge(s_lgc, q + 1)
                transposed(6, xh[par], n).then_inc(s_xft, 1)
                pe.wait_ge(s_xftc, q + 1)
                for j in range(n):
                    for kt in range(KT):
                        m = MM(PS[:, 6, j * NE:(j + 1) * NE], fg["xft"][:, kt, j * P:(j + 1) * P],
                               fr["wr"][:, kt, :], start=kt == 0, stop=kt == KT - 1)
                m.then_inc(s_lg, 1)

            by_group(pe, pe_first, pe_second, pe_third)

            pe.wait_ge(s_ecnt, 1)
            MM(PS[:, 0, 0:NE], lower[:, :], fb_["cnt"], start=True, stop=True)
            MM(PS[:, 0, 64:64 + NE], ones[:, :], fb_["cnt"], start=True, stop=True).then_inc(s_etot, 1)
            pe.sem_inc(s_eused, 1)
            pe.wait_ge(s_eoh, 1)
            MM(PS[:, 0, 0:2 * NCE], z16[:, :], iota_c[:, 0:2 * NCE], start=True, stop=False)
            with pe.Fori(0, NK // CE7) as i:
                pe.wait_ge(s_eopen, i + 1)
                pe.wait_ge(s_eohv, i + 1)
                for k in range(CE7):
                    m = MM(PS[:, 0, 0:2 * NCE], fc["ohs"][:, k, :], fc["ohv"][:, k, :, :].rearrange("p f c -> p (f c)"),
                           start=False, stop=False)
                m.then_inc(s_eused, 1)
            MM(PS[:, 0, 0:2 * NCE], z16[:, :], iota_c[:, 0:2 * NCE], start=False, stop=True).then_inc(s_esort, 1)

            def load_experts(ap):
                return nc.values_load_multi_w_load_instructions(
                    ap, engines=(mybir.EngineType.PE,), min_val=0, max_val=NE - 1,
                    skip_runtime_bounds_check_because="computed on the chip as a minimum with NE - 1")[1]

            def turn_x(k, count):
                pe.wait_ge(s_g[k % ER], XG0 + count)
                for kt in range(KT):
                    m = TR(PS[:, k % 2, kt * P:(kt + 1) * P], fe["xg"][:, k % ER, kt * P:(kt + 1) * P], ident[:, :])
                m.then_inc(s_t1e, 1)

            def up(k, count, e):
                pe.wait_ge(s_c1, count)
                for kt in range(KT):
                    m = MM(PS[:, 2 + k % 2, :], xT[:, k % 2, kt * P:(kt + 1) * P],
                           fr["w1"][:, ds(e, 1), kt, :].rearrange("p a f -> p (a f)"), start=kt == 0, stop=kt == KT - 1)
                m.then_inc(s_up, 1)

            pe.wait_ge(s_ready, 1)
            pe.sem_inc(s_b2, 2)
            e0 = load_experts(sm["eid"][0:1, 0:1])[0]
            turn_x(0, 16)
            turn_x(1, 16)
            up(0, 1, e0)
            with pe.Fori(0, NCE // ER) as i:
                es = load_experts(sm["eid"][0:1, ds(i * ER, ER + 1)])
                for k in range(ER):
                    w = i * ER + k
                    pe.wait_ge(s_ge, w + 1)
                    for t in range(HT):
                        m = TR(PS[:, 4 + k % 2, t * P:(t + 1) * P], fe["h"][:, k % 2, t * P:(t + 1) * P], ident[:, :])
                    m.then_inc(s_t2, 1)
                    turn_x(k + 2, i * 16 + (16 if k + 2 < ER else 32))
                    up(k + 1, w + 2, es[k + 1])
                    pe.wait_ge(s_c2, w + 1)
                    pe.wait_ge(s_b2, w + 1)
                    for t in range(HT):
                        m = MM(PS[:, 6 + k % 2, 0:F], fe["hT"][:, k % 2, t * P:(t + 1) * P],
                               fa_["w2"][:, ds(es[k], 1), t, :].rearrange("p a f -> p (a f)"), start=t == 0, stop=t == HT - 1)
                    m.then_inc(s_dn, 1)


_INS = ['x', 'src', 'dst', 'L0_gnn_W1', 'L0_gnn_b1', 'L0_gnn_W2', 'L0_gnn_b2', 'L0_gnn_a', 'L0_mix_Wqkv',
        'L0_mix_Wout', 'L0_mix_bout', 'L0_ffn_gamma', 'L0_ffn_beta', 'L0_ffn_Wr', 'L0_ffn_br', 'L0_ffn_W1',
        'L0_ffn_b1', 'L0_ffn_W2', 'L0_ffn_b2']


def kernel(**inputs):
    import numpy as np
    import concourse.bacc as bacc
    from concourse.bass_utils import run_bass_kernel_spmd

    nc = bacc.Bacc("TRN2", target_bir_lowering=False, num_devices=1)
    arrays, args = {}, []
    for name in _INS:
        a = np.ascontiguousarray(inputs[name])
        arrays[f"in_{name}"] = a
        args.append(nc.dram_tensor(f"in_{name}", a.shape, mybir.dt.from_np(a.dtype), kind="ExternalInput").ap())
    out = nc.dram_tensor("out_0", inputs['x'].shape, mybir.dt.float32, kind="ExternalOutput").ap()
    gps_layer(nc, *args, out)
    return run_bass_kernel_spmd(nc, [arrays], core_ids=[0]).results[0]["out_0"]
```
